# Optimizing a Trainium2 kernel written in Bass

```python
import numpy as np
import jax
import jax.numpy as jnp

def _softmax(x, axis=-1):
    return jax.nn.softmax(x, axis=axis)

def _gelu(x):
    return jax.nn.gelu(x, approximate=True)

def _silu(x):
    return jax.nn.silu(x)

def _sigmoid(x):
    return jax.nn.sigmoid(x)

def _layernorm(x, axis=-1, eps=1e-05):
    m = jnp.mean(x, axis=axis, keepdims=True)
    v = jnp.var(x, axis=axis, keepdims=True)
    return (x - m) / jnp.sqrt(v + eps)

def _scatter_add(tgt, idx, src, axis=0):
    return tgt.at[idx].add(src)

def _segment_sum(src, seg, n):
    return jax.ops.segment_sum(src, seg, n)
kernel_name = 'mk_cond_resid_d4_seqx_r4_3834bb'

def setup_inputs(seed: int=0):
    np.random.seed(seed)
    _w = jnp.asarray

    def _rec_inputs():
        import jax
        import jax.numpy as jnp
        _rk = jax.random.key(seed)
        x = -0.000125 + 0.9999 * jax.random.normal(jax.random.fold_in(_rk, 1), (32, 256, 256), jnp.float32)
        _lenS = 256 - jax.random.randint(jax.random.fold_in(_rk, 7), (32,), 0, max(1, 256 // 4) + 1, jnp.int32)
        _lenS2 = 256 - jax.random.randint(jax.random.fold_in(_rk, 8), (32,), 0, max(1, 256 // 4) + 1, jnp.int32)
        cond_1024 = -0.00493535 + 1.00056 * jax.random.normal(jax.random.fold_in(_rk, 11), (32, 256), jnp.float32)
        return (x, cond_1024)
    x, cond_1024 = _rec_inputs()

    def _L0_cond_setup():
        import jax, jax.numpy as jnp
        import numpy as np
        key = jax.random.key(seed)
        k1, k2, k3, k4 = jax.random.split(key, 4)
        B, T, I, H = (64, 128, 256, 256)
        X = jax.random.normal(k1, (B, T, I), dtype=jnp.float32)
        hs = jax.random.normal(k2, (B, H), dtype=jnp.float32)
        Wx = jax.random.normal(k3, (H, I), dtype=jnp.float32) * 0.02
        Wh = jax.random.normal(k4, (H, H), dtype=jnp.float32) * 0.02
        return {'X': X, 'hs': hs, 'Wx': Wx, 'Wh': Wh}
    _L0_cond_all = _L0_cond_setup()
    _L0_cond_in = {k: v for k, v in _L0_cond_all.items() if k in ('Wx', 'Wh')}
    del _L0_cond_all

    def _L1_cond_setup():
        import jax, jax.numpy as jnp
        import numpy as np
        from jax import lax
        ALPHA_LO = float(np.exp(-1.0 / 5.0))
        ALPHA_HI = float(np.exp(-1.0 / 25.0))
        THRESHOLD = 1.0

        @jax.custom_vjp
        def spike_boxcar(x):
            return (x > 0).astype(x.dtype)

        def _spike_fwd(x):
            return (spike_boxcar(x), x)

        def _spike_bwd(x, g):
            mask = ((x > -0.5) & (x <= 0.5)).astype(g.dtype)
            return (g * mask,)
        spike_boxcar.defvjp(_spike_fwd, _spike_bwd)
        key = jax.random.key(seed)
        kx, kW, kV, ka, ku, ks = jax.random.split(key, 6)
        B, T, I, H = (64, 250, 256, 256)
        x = jax.random.normal(kx, (B, T, I), dtype=jnp.float32)
        W = jax.random.normal(kW, (H, I), dtype=jnp.float32) / np.sqrt(I)
        V = jnp.linalg.qr(jax.random.normal(kV, (H, H), dtype=jnp.float32))[0]
        alpha = jax.random.uniform(ka, (H,), dtype=jnp.float32, minval=ALPHA_LO, maxval=ALPHA_HI)
        ut0 = jax.random.uniform(ku, (B, H), dtype=jnp.float32)
        st0 = jax.random.uniform(ks, (B, H), dtype=jnp.float32)
        return {'x': x, 'W': W, 'V': V, 'alpha': alpha, 'ut0': ut0, 'st0': st0}
    _L1_cond_all = _L1_cond_setup()
    _L1_cond_in = {k: v for k, v in _L1_cond_all.items() if k in ('W', 'V', 'alpha')}
    del _L1_cond_all

    def _L2_cond_setup():
        import jax, jax.numpy as jnp
        import numpy as np
        D_MODEL = 256
        D_FF = 1024
        N_EXPERTS = 8
        TOP_K = 2
        N_SHARED = 2
        B, T = (4, 512)
        key = jax.random.key(seed)
        ks = jax.random.split(key, 9)
        Hs = D_FF // 2
        Hr = D_FF // 4
        inp = {'x': jax.random.normal(ks[0], (B, T, D_MODEL), dtype=jnp.float32), 't_emb': jax.random.normal(ks[1], (B, D_MODEL), dtype=jnp.float32), 'W_router': 0.01 * jax.random.normal(ks[2], (N_EXPERTS, 2 * D_MODEL), dtype=jnp.float32), 'router_bias': jnp.zeros((N_EXPERTS,), dtype=jnp.float32), 's_w1': 0.02 * jax.random.normal(ks[3], (N_SHARED, Hs, D_MODEL), dtype=jnp.float32), 's_w3': 0.02 * jax.random.normal(ks[4], (N_SHARED, Hs, D_MODEL), dtype=jnp.float32), 's_w2': 0.02 * jax.random.normal(ks[5], (N_SHARED, D_MODEL, Hs), dtype=jnp.float32), 'r_w1': 0.02 * jax.random.normal(ks[6], (N_EXPERTS, Hr, D_MODEL), dtype=jnp.float32), 'r_w2': 0.02 * jax.random.normal(ks[7], (N_EXPERTS, D_MODEL, Hr), dtype=jnp.float32)}
        return inp
    _L2_cond_all = _L2_cond_setup()
    _L2_cond_in = {k: v for k, v in _L2_cond_all.items() if k in ('W_router', 'router_bias', 's_w1', 's_w3', 's_w2', 'r_w1', 'r_w2')}
    del _L2_cond_all

    def _L3_cond_setup():
        import jax, jax.numpy as jnp
        import numpy as np
        key = jax.random.key(seed)
        ks = jax.random.split(key, 8)
        B, L, D, N, K = (4, 1024, 256, 64, 4)
        return {'x': jax.random.normal(ks[0], (B, L, D), dtype=jnp.float32), 'conv_w': jax.random.normal(ks[1], (K, 1, D), dtype=jnp.float32) * 0.1, 'conv_b': jnp.zeros((D,), dtype=jnp.float32), 'Wp': jax.random.normal(ks[2], (D, 2 * N), dtype=jnp.float32) * (1.0 / np.sqrt(D)), 'bp': jnp.zeros((2 * N,), dtype=jnp.float32), 'Ws': jax.random.normal(ks[3], (D, N), dtype=jnp.float32) * (1.0 / np.sqrt(D)), 'bs': jnp.zeros((N,), dtype=jnp.float32), 'A_log': jax.random.normal(ks[4], (N,), dtype=jnp.float32) * 0.02, 'dt_log': jax.random.normal(ks[5], (N,), dtype=jnp.float32) * 0.02, 'Wo': jax.random.normal(ks[6], (N, D), dtype=jnp.float32) * (1.0 / np.sqrt(N)), 'bo': jnp.zeros((D,), dtype=jnp.float32)}
    _L3_cond_all = _L3_cond_setup()
    _L3_cond_in = {k: v for k, v in _L3_cond_all.items() if k in ('conv_b', 'Wp', 'bp', 'Ws', 'bs', 'A_log', 'dt_log', 'Wo', 'bo')}
    del _L3_cond_all
    return {'x': x, 'cond_1024': cond_1024, 'L0_cond_Wx': _L0_cond_in['Wx'], 'L0_cond_Wh': _L0_cond_in['Wh'], 'L1_cond_W': _L1_cond_in['W'], 'L1_cond_V': _L1_cond_in['V'], 'L1_cond_alpha': _L1_cond_in['alpha'], 'L2_cond_W_router': _L2_cond_in['W_router'], 'L2_cond_router_bias': _L2_cond_in['router_bias'], 'L2_cond_s_w1': _L2_cond_in['s_w1'], 'L2_cond_s_w3': _L2_cond_in['s_w3'], 'L2_cond_s_w2': _L2_cond_in['s_w2'], 'L2_cond_r_w1': _L2_cond_in['r_w1'], 'L2_cond_r_w2': _L2_cond_in['r_w2'], 'L3_cond_conv_b': _L3_cond_in['conv_b'], 'L3_cond_Wp': _L3_cond_in['Wp'], 'L3_cond_bp': _L3_cond_in['bp'], 'L3_cond_Ws': _L3_cond_in['Ws'], 'L3_cond_bs': _L3_cond_in['bs'], 'L3_cond_A_log': _L3_cond_in['A_log'], 'L3_cond_dt_log': _L3_cond_in['dt_log'], 'L3_cond_Wo': _L3_cond_in['Wo'], 'L3_cond_bo': _L3_cond_in['bo']}

def reference(x, cond_1024, L0_cond_Wx, L0_cond_Wh, L1_cond_W, L1_cond_V, L1_cond_alpha, L2_cond_W_router, L2_cond_router_bias, L2_cond_s_w1, L2_cond_s_w3, L2_cond_s_w2, L2_cond_r_w1, L2_cond_r_w2, L3_cond_conv_b, L3_cond_Wp, L3_cond_bp, L3_cond_Ws, L3_cond_bs, L3_cond_A_log, L3_cond_dt_log, L3_cond_Wo, L3_cond_bo):
    import jax
    import jax.numpy as jnp

    def _L0_cond_ref(X, hs, Wx, Wh):
        import jax, jax.numpy as jnp
        import numpy as np

        def step(h, x_t):
            h_next = jnp.tanh(x_t @ Wx.T + h @ Wh.T)
            return (h_next, h)
        _, hs_seq = jax.lax.scan(step, hs, jnp.swapaxes(X, 0, 1))
        return jnp.swapaxes(hs_seq, 0, 1)

    def _L1_cond_ref(x, W, V, alpha, ut0, st0):
        import jax, jax.numpy as jnp
        import numpy as np
        from jax import lax
        ALPHA_LO = float(np.exp(-1.0 / 5.0))
        ALPHA_HI = float(np.exp(-1.0 / 25.0))
        THRESHOLD = 1.0

        @jax.custom_vjp
        def spike_boxcar(x):
            return (x > 0).astype(x.dtype)

        def _spike_fwd(x):
            return (spike_boxcar(x), x)

        def _spike_bwd(x, g):
            mask = ((x > -0.5) & (x <= 0.5)).astype(g.dtype)
            return (g * mask,)
        spike_boxcar.defvjp(_spike_fwd, _spike_bwd)
        Wx = jnp.einsum('bti,hi->bth', x, W)
        a = jnp.clip(alpha, ALPHA_LO, ALPHA_HI)
        H = V.shape[0]
        Vz = V * (1.0 - jnp.eye(H, dtype=V.dtype))

        def step(carry, wx_t):
            ut, st = carry
            ut = a * (ut - st) + (1.0 - a) * (wx_t + st @ Vz)
            st = spike_boxcar(ut - THRESHOLD)
            return ((ut, st), st)
        Wx_t = jnp.swapaxes(Wx, 0, 1)
        _, s = lax.scan(step, (ut0, st0), Wx_t)
        return jnp.swapaxes(s, 0, 1)

    def _L2_cond_ref(x, t_emb, W_router, router_bias, s_w1, s_w3, s_w2, r_w1, r_w2):
        import jax, jax.numpy as jnp
        import numpy as np
        D_MODEL = 256
        D_FF = 1024
        N_EXPERTS = 8
        TOP_K = 2
        N_SHARED = 2
        B, T = (4, 512)
        Bn, Tn, C = x.shape
        N = Bn * Tn
        x_flat = x.reshape(N, C)
        t_flat = jnp.broadcast_to(t_emb[:, None, :], (Bn, Tn, C)).reshape(N, C)
        shared_out = jnp.zeros_like(x_flat)
        for e in range(N_SHARED):
            h = jax.nn.silu(x_flat @ s_w1[e].T) * (x_flat @ s_w3[e].T)
            shared_out = shared_out + h @ s_w2[e].T
        shared_out = shared_out / N_SHARED
        router_in = jnp.concatenate([x_flat, t_flat], axis=-1)
        s = jax.nn.sigmoid((router_in @ W_router.T).astype(jnp.float32))
        sel_scores = s + router_bias
        _, topk_idx = jax.lax.top_k(sel_scores, TOP_K)
        s_sel = jnp.take_along_axis(s, topk_idx, axis=1)
        denom = jnp.sum(s_sel, axis=1, keepdims=True)
        gates = jnp.where(denom > 1e-09, s_sel / (denom + 1e-09), 1.0 / TOP_K).astype(x.dtype)
        gates_full = jnp.sum(jax.nn.one_hot(topk_idx, N_EXPERTS, dtype=x.dtype) * gates[..., None], axis=1)
        routed_out = jnp.zeros_like(x_flat)
        for e in range(N_EXPERTS):
            h = jax.nn.gelu(x_flat @ r_w1[e].T, approximate=False)
            routed_out = routed_out + h @ r_w2[e].T * gates_full[:, e:e + 1]
        out = (shared_out + routed_out) / (N_SHARED + TOP_K)
        return out.reshape(Bn, Tn, C)

    def _L3_cond_ref(x, conv_w, conv_b, Wp, bp, Ws, bs, A_log, dt_log, Wo, bo):
        import jax, jax.numpy as jnp
        import numpy as np
        B, L, D = x.shape
        K = conv_w.shape[0]
        N = Ws.shape[1]
        x_pad = jnp.pad(x, ((0, 0), (K - 1, 0), (0, 0)))
        conv = conv_b + sum((x_pad[:, k:k + L, :] * conv_w[k, 0] for k in range(K)))
        proj = conv @ Wp + bp
        B_t = jax.nn.softplus(proj[..., :N])
        C_t = jnp.tanh(proj[..., N:])
        u = x @ Ws + bs
        A = -jax.nn.softplus(A_log)
        dt = jax.nn.softplus(dt_log)
        decay = 1.0 + dt * A

        def step(state, inputs):
            u_t, b_t, c_t = inputs
            state = decay * state + dt * b_t * u_t
            return (state, c_t * state)
        init = jnp.zeros((B, N), dtype=x.dtype)
        xs = tuple((jnp.swapaxes(a, 0, 1) for a in (u, B_t, C_t)))
        _, ys = jax.lax.scan(step, init, xs, unroll=4)
        y = jnp.swapaxes(ys, 0, 1)
        return y @ Wo + bo
    x = x + _L0_cond_ref(x, cond_1024, L0_cond_Wx, L0_cond_Wh)
    x = x + _L1_cond_ref(x, L1_cond_W, L1_cond_V, L1_cond_alpha, cond_1024, cond_1024)
    x = x + _L2_cond_ref(x, cond_1024, L2_cond_W_router, L2_cond_router_bias, L2_cond_s_w1, L2_cond_s_w3, L2_cond_s_w2, L2_cond_r_w1, L2_cond_r_w2)
    x = x + _L3_cond_ref(x, cond_1024[:, None, :], L3_cond_conv_b, L3_cond_Wp, L3_cond_bp, L3_cond_Ws, L3_cond_bs, L3_cond_A_log, L3_cond_dt_log, L3_cond_Wo, L3_cond_bo)
    return x

_drawn_inputs = setup_inputs


def setup_inputs(seed=0):
    import zlib

    import numpy as np

    out = dict(_drawn_inputs(seed))
    spreads = {'L2_cond_router_bias': (0.0, 0.334),
     'L3_cond_conv_b': (0.0, 0.1),
     'L3_cond_bp': (0.0, 0.288),
     'L3_cond_bs': (0.0, 0.1),
     'L3_cond_bo': (0.0, 0.554)}
    factors = {'L1_cond_V': 8.0,
     'L2_cond_W_router': 4.022,
     'L2_cond_s_w1': 5.747,
     'L2_cond_s_w3': 5.64,
     'L2_cond_s_w2': 5.716,
     'L2_cond_r_w1': 2.674,
     'L3_cond_A_log': 5.662,
     'L3_cond_dt_log': 4.039}
    for name, (base, spread) in spreads.items():
        noise = np.random.default_rng([zlib.crc32(name.encode()), seed]).standard_normal(out[name].shape)
        drawn = base * np.exp(spread * noise) if base else spread * noise
        out[name] = jnp.asarray(drawn.astype(out[name].dtype))
    for name, factor in factors.items():
        out[name] = (out[name] * factor).astype(out[name].dtype)
    return out
```

```python
from contextlib import ExitStack

import concourse.bass as bass
from concourse import mybir

ALU = mybir.AluOpType
ACT = mybir.ActivationFunctionType
AX_X = mybir.AxisListType.X
F32 = mybir.dt.float32
F16 = mybir.dt.float16
U32 = mybir.dt.uint32

P = 128
B, T, D = 32, 256, 256
KD = D // P
N_SHARED, FF_SHARED = 2, 512
N_ROUTED, FF_ROUTED = 8, 256
N_STATE = 64
TAPS = B

STEPS = 8
TOK = STEPS * B
CHUNKS = T // STEPS
PAIRS = CHUNKS // 2
PAIR = 2 * TOK
HIST = (TAPS - 1) * B
QB = TOK // P

SHARED_UNITS = N_SHARED * FF_SHARED // (2 * P)
UNITS = SHARED_UNITS + N_ROUTED
BANKS = 4
LAG = 3
CHAIN_AT = 2

W_SCALE = 64.0
H_SCALE = 16.0
Y_SCALE = 1.0 / (W_SCALE * H_SCALE)
LAYER = 4.0

GATE_OPS = 22
TAP_OPS = KD * TAPS
POST_OPS = 5

_SMALL = [
    ("wx", KD * D), ("wh", KD * D), ("cond", KD * B), ("alpha_col", KD * B),
    ("w", KD * D), ("v", KD * D), ("off_diag", KD * D), ("alpha_row", D),
    ("cond4", KD * P), ("router", 2 * KD * N_ROUTED), ("router_bias", QB * N_ROUTED),
    ("iota", N_ROUTED), ("proj", KD * 2 * N_STATE), ("skip", KD * N_STATE), ("out", D),
    ("proj_bias", 1), ("skip_bias", 1), ("out_bias", KD), ("conv_bias", KD),
    ("logs", 2),
]
SMALL = {}
_at = 0
for _n, _w in _SMALL:
    SMALL[_n] = (_at, _w)
    _at += _w
SMALL_COLS = _at
FIRST_COLS = SMALL["w"][0]

SW1, SW3, SW2 = 0, 2048, 4096
RW1 = 6144
RW2 = RW1 + N_ROUTED * KD * FF_ROUTED
BIG_COLS = RW2 + N_ROUTED * KD * FF_ROUTED
STAGE = 2048
STAGES = BIG_COLS // STAGE

A_LO = 0.8187307530779818
A_HI = 0.9607894391523232


def last_user(m):
    use = lambda j: 2 * j + 1 if j < SHARED_UNITS else SHARED_UNITS + j
    before = use(m) - BANKS
    if before < 0:
        before += 2 * SHARED_UNITS + N_ROUTED
        return (before // 2 if before < 2 * SHARED_UNITS else before - SHARED_UNITS) - UNITS
    return before // 2 if before < 2 * SHARED_UNITS else before - SHARED_UNITS


def taps_at(slot):
    first, n = 5, 2 * UNITS - 5
    at = lambda j: max(0, min(TAP_OPS, TAP_OPS * j // n))
    return range(at(slot - first), at(slot - first + 1))


class Turn:

    def __init__(self, i):
        self.i = i

    def chunk(self, offset):
        return self.i * 2 + offset

    def has(self, offset):
        return not isinstance(self.i, int) or 0 <= 2 * self.i + offset < CHUNKS

    def at(self, i):
        return isinstance(self.i, int) and self.i == i

    def has_pair(self, offset):
        return not isinstance(self.i, int) or 0 <= self.i + offset < PAIRS


FIRST_TURN, LAST_TURN = 3, PAIRS - 1
TURNS = PAIRS + 3


def run_turns(engine, body, first=FIRST_TURN, last=LAST_TURN):
    for i in range(first):
        body(Turn(i))
    with engine.Fori(first, last + 1) as i:
        body(Turn(i))
    for i in range(last + 1, TURNS):
        body(Turn(i))


def wait(engine, sem, value):
    if not isinstance(value, int) or value > 0:
        engine.wait_ge(sem, value)


def build(nc: bass.Bass, x_t: bass.AP, small_w: bass.AP, big_w: bass.AP, out_t: bass.AP, gates_dram: bass.AP):
    with ExitStack() as ctx:
        def sb(name, shape, dt=F32):
            return ctx.enter_context(nc.sbuf_tensor(name, shape, dt))

        def psum(name, shape):
            return ctx.enter_context(nc.psum_tensor(name, shape, F32))

        def sem(name):
            return ctx.enter_context(nc.semaphore(name))

        small = sb("small", [P, SMALL_COLS])

        def part(name, **axes):
            at, w = SMALL[name]
            ap = small[:, at:at + w]
            if not axes:
                return ap
            names = " ".join(axes)
            first = next(iter(axes))
            return ap.rearrange(f"p ({names}) -> p {names}", **{first: axes[first]})

        wx, wh = part("wx", k=KD, n=D), part("wh", k=KD, n=D)
        cond = part("cond", k=KD, b=B)
        alpha_col = part("alpha_col", k=KD, b=B)
        w_in, v_in, off_diag = part("w", k=KD, n=D), part("v", k=KD, n=D), part("off_diag", k=KD, n=D)
        alpha_row = part("alpha_row")
        cond4 = part("cond4", k=KD, n=P)
        router = part("router", k=2 * KD, e=N_ROUTED)
        router_bias = part("router_bias", q=QB, e=N_ROUTED)
        iota = part("iota")
        proj, skip = part("proj", k=KD, n=2 * N_STATE), part("skip", k=KD, n=N_STATE)
        w_out = part("out")
        proj_bias, skip_bias = part("proj_bias"), part("skip_bias")
        out_bias, conv_bias = part("out_bias"), part("conv_bias")
        logs = part("logs")

        stage = sb("stage", [P, 2, STAGE])
        w_hi = sb("w_hi", [P, BIG_COLS], F16)
        w_lo = sb("w_lo", [P, BIG_COLS], F16)
        w_spike = sb("w_spike", [P, KD, D])
        v_hi = sb("v_hi", [P, KD, D], F16)
        v_lo = sb("v_lo", [P, KD, D], F16)
        keep_row = sb("keep_row", [P, D])
        neg_a = sb("neg_a", [P, KD, B])
        cond_hi = sb("cond_hi", [P, KD, B], F16)
        cond_lo = sb("cond_lo", [P, KD, B], F16)
        cond_logits = sb("cond_logits", [P, N_ROUTED])
        state_abs = sb("state_abs", [N_STATE, 2])
        state_exp = sb("state_exp", [N_STATE, 2])
        state_ln = sb("state_ln", [N_STATE, 2])
        state_sp = sb("state_sp", [N_STATE, 2])
        step_a = sb("step_a", [N_STATE, 1])
        decay = sb("decay", [N_STATE, 1])
        decay_run = sb("decay_run", [N_STATE, B, 2 * STEPS])
        w_out_dt = sb("w_out_dt", [N_STATE, D])

        x_in = [sb(f"x_in{p}", [P, KD, TOK]) for p in range(2)]
        h_rnn = [sb(f"h_rnn{p}", [P, KD, TOK]) for p in range(2)]
        x1 = [sb(f"x1_{p}", [P, KD, TOK]) for p in range(2)]
        u_mem = sb("u_mem", [P, KD, B])
        excess = sb("excess", [P, KD, B])
        leak = sb("leak", [P, KD, B])
        spikes = [sb(f"spikes{p}", [P, KD, TOK], F16) for p in range(2)]
        x2 = [sb(f"x2_{p}", [P, KD, TOK]) for p in range(2)]
        x2_hi = [sb(f"x2_hi{p}", [P, KD, TOK], F16) for p in range(2)]
        x2_lo = [sb(f"x2_lo{p}", [P, KD, TOK], F16) for p in range(2)]
        act_f = [sb(f"act_f{j}", [P, 2, TOK]) for j in range(2)]
        silu = [sb(f"silu{j}", [P, 2, TOK]) for j in range(2)]
        hid = [sb(f"hid{j}", [P, 2, TOK]) for j in range(2)]
        hid_hi = [sb(f"hid_hi{j}", [P, 2, TOK], F16) for j in range(4)]
        hid_lo = [sb(f"hid_lo{j}", [P, 2, TOK], F16) for j in range(4)]
        gates = [sb(f"gates{p}", [P, QB, N_ROUTED]) for p in range(2)]
        gates_all = [sb(f"gates_all{p}", [P, TOK, N_ROUTED]) for p in range(2)]
        logits = sb("logits", [P, QB, N_ROUTED])
        half_scores = sb("half_scores", [P, QB, N_ROUTED])
        scores = sb("scores", [P, QB, N_ROUTED])
        select = sb("select", [P, QB, N_ROUTED])
        dve_hold = sb("dve_hold", [P, 1])
        pool_hold = sb("pool_hold", [P, 1])
        top = sb("top", [P, QB, 8])
        top_at = sb("top_at", [P, QB, 8], U32)
        top_at_f = sb("top_at_f", [P, QB, 2])
        chosen0 = sb("chosen0", [P, QB, N_ROUTED])
        chosen = sb("chosen", [P, QB, N_ROUTED])
        picked = sb("picked", [P, QB, N_ROUTED])
        denom = sb("denom", [P, QB])
        denom_eps = sb("denom_eps", [P, QB])
        denom_inv = sb("denom_inv", [P, QB])
        denom_ok = sb("denom_ok", [P, QB])
        gate_scale = sb("gate_scale", [P, QB])
        gate_even = sb("gate_even", [P, QB])
        gate_a = sb("gate_a", [P, QB, N_ROUTED])
        x3_new = sb("x3_new", [P, KD, PAIR])
        hist = sb("hist", [P, KD, HIST + PAIR])
        conv = sb("conv", [P, KD, PAIR])
        z_b = sb("z_b", [N_STATE, PAIR])
        c_t = sb("c_t", [N_STATE, PAIR])
        u_t = sb("u_t", [N_STATE, PAIR])
        z_abs = sb("z_abs", [N_STATE, PAIR])
        z_exp = sb("z_exp", [N_STATE, PAIR])
        z_ln = sb("z_ln", [N_STATE, PAIR])
        b_t = sb("b_t", [N_STATE, PAIR])
        drive = sb("drive", [N_STATE, B, 2 * STEPS])
        state = sb("state", [N_STATE, B, 2 * STEPS])
        y_t = sb("y_t", [N_STATE, PAIR])
        out_sb = [sb(f"out_sb{q}", [P, KD, TOK]) for q in range(2)]

        ps_rnn = psum("ps_rnn", [P, KD, TOK])
        ps_spike = psum("ps_spike", [P, KD, TOK])
        ps_y = psum("ps_y", [P, KD, TOK])
        ps_misc = psum("ps_misc", [P, KD, TOK])
        ps_hid = [psum(f"ps_hid{j}", [P, 2, TOK]) for j in range(BANKS)]

        first_loaded, small_loaded = sem("first_loaded"), sem("small_loaded")
        stage_loaded = [sem(f"stage_loaded{j}") for j in range(2)]
        stage_hi, stage_lo = sem("stage_hi"), sem("stage_lo")
        h_start, pool_start = sem("h_start"), sem("pool_start")
        prep, prep_act, cond_mm = sem("prep"), sem("prep_act"), sem("cond_mm")
        x_loaded = [sem(f"x_loaded{p}") for p in range(2)]
        rnn_sums, h_ready, x1_done = sem("rnn_sums"), sem("h_ready"), sem("x1_done")
        spike_sums, membrane, spiked = sem("spike_sums"), sem("membrane"), sem("spiked")
        excess_done, leak_done = sem("excess_done"), sem("leak_done")
        x2_done, x2_hi_done, x2_lo_done = sem("x2_done"), sem("x2_hi_done"), sem("x2_lo_done")
        router_sums, gate_ops, scored = sem("router_sums"), sem("gate_ops"), sem("scored")
        gates_stored = sem("gates_stored")
        gates_loaded = [sem(f"gates_loaded{p}") for p in range(2)]
        hidden, activated, silu_done = sem("hidden"), sem("activated"), sem("silu_done")
        evacuated, gated = sem("evacuated"), sem("gated")
        hi_done, lo_done, summed = sem("hi_done"), sem("lo_done"), sem("summed")
        x3_done, hist_half, hist_ready = sem("x3_done"), sem("hist_half"), sem("hist_ready")
        taps_done = sem("taps_done")
        post_sums, post_copied, post_act = sem("post_sums"), sem("post_copied"), sem("post_act")
        post_ops, out_sums, out_done = sem("post_ops"), sem("out_sums"), sem("out_done")
        out_stored = sem("out_stored")

        cols = [slice(s * B, (s + 1) * B) for s in range(STEPS)]
        halves = [slice(q * TOK, (q + 1) * TOK) for q in range(2)]
        PREP_OPS = 15
        block = ctx.enter_context(nc.Block())

        @block.sync
        def _(sp):
            sp.dma_start(small[:, 0:FIRST_COLS], small_w[:, 0:FIRST_COLS]).then_inc(first_loaded, 16)
            for c in range(2):
                sp.dma_start(x_in[c][:], x_t[:, :, c * TOK:(c + 1) * TOK]).then_inc(x_loaded[c], 16)
            sp.dma_start(small[:, FIRST_COLS:], small_w[:, FIRST_COLS:]).then_inc(small_loaded, 16)
            for j in range(STAGES):
                if j >= 2:
                    sp.wait_ge(stage_hi, j - 1)
                    sp.wait_ge(stage_lo, j - 1)
                sp.dma_start(stage[:, j % 2, :], big_w[:, j * STAGE:(j + 1) * STAGE]).then_inc(stage_loaded[j % 2], 16)

            def turn(t):
                for hf in range(2):
                    if t.has(hf - 2):
                        c = t.chunk(hf - 2)
                        sp.wait_ge(gate_ops, GATE_OPS * (c + 1))
                        sp.dma_start(gates_dram[hf].rearrange("(q p) e -> p q e", p=P), gates[hf][:]).then_inc(gates_stored, 16)
                        sp.wait_ge(gates_stored, 16 * (c + 1))
                        wait(sp, gated, N_ROUTED * (c - 1))
                        sp.dma_start(gates_all[hf][:], gates_dram[hf].rearrange("(o n) e -> o n e", o=1).broadcast_to((P, TOK, N_ROUTED))).then_inc(gates_loaded[hf], 16)
                    if hf == 0 and t.has_pair(-3):
                        for q in range(2):
                            n = t.chunk(q - 6)
                            sp.wait_ge(out_done, KD * (n + 1))
                            sp.dma_start(out_t[:, :, bass.ds(n * TOK, TOK)], out_sb[q][:]).then_inc(out_stored, 16)
                    if t.has(hf) and t.has(hf + 2):
                        c = t.chunk(hf)
                        sp.wait_ge(x1_done, c + 1)
                        sp.dma_start(x_in[hf][:], x_t[:, :, bass.ds((c + 2) * TOK, TOK)]).then_inc(x_loaded[hf], 16)

            run_turns(sp, turn, last=LAST_TURN - 1)
            sp.wait_ge(out_stored, 16 * CHUNKS)

        @block.tensor
        def _(pe):
            PASSES = ((0, 0), (0, 1), (1, 0))

            def products(out, pairs, first=True):
                last = None
                for j, (w, v) in enumerate(pairs):
                    last = nc.tensor.matmul(out, w, v, start=first and j == 0, stop=j == len(pairs) - 1, skip_group_check=True)
                return last

            def project(ps, weights, data):
                for mt in range(KD):
                    products(ps[:, mt, :], [(weights[:, k, mt * P:(mt + 1) * P], data[:, k, :]) for k in range(KD)], first=mt == 0)

            def unit_hidden(c, m, par):
                before = last_user(m)
                if before % UNITS < SHARED_UNITS:
                    wait(pe, evacuated, SHARED_UNITS * (c + before // UNITS) + before % UNITS + 1)
                else:
                    wait(pe, activated, UNITS * c + before + 1)
                split = (x2_hi[par], x2_lo[par])
                w = (w_hi, w_lo)
                if m < SHARED_UNITS:
                    e, part_ = m // 2, m % 2
                    jobs = [(ps_hid[(2 * m + j) % BANKS], base + e * KD * FF_SHARED + part_ * 2 * P, FF_SHARED)
                            for j, base in enumerate((SW1, SW3))]
                else:
                    e = m - SHARED_UNITS
                    jobs = [(ps_hid[(SHARED_UNITS + m) % BANKS], RW1 + e * KD * FF_ROUTED, FF_ROUTED)]
                for ps, base, ff in jobs:
                    for ft in range(2):
                        last = products(ps[:, ft, :], [
                            (w[a][:, base + k * ff + ft * P:base + k * ff + (ft + 1) * P], split[b][:, k, :])
                            for k in range(KD) for a, b in PASSES], first=ft == 0)
                last.then_inc(hidden, 1)

            def unit_output(c, m):
                pe.wait_ge(lo_done, UNITS * c + m + 1)
                if m == 0:
                    wait(pe, x3_done, c)
                split = (hid_hi[m % 4], hid_lo[m % 4])
                w = (w_hi, w_lo)
                base = SW2 + m * 2 * D if m < SHARED_UNITS else RW2 + (m - SHARED_UNITS) * KD * D
                for mt in range(KD):
                    last = products(ps_y[:, mt, :], [
                        (w[a][:, base + f * D + mt * P:base + f * D + (mt + 1) * P], split[b][:, f, :])
                        for f in range(2) for a, b in PASSES], first=m == 0 and mt == 0)
                last.then_inc(summed, 1)

            pe.wait_ge(small_loaded, 16)
            products(ps_misc[:, 0, 0:N_ROUTED], [(cond4[:, k, :], router[:, KD + k, :]) for k in range(KD)]).then_inc(cond_mm, 1)
            pe.wait_ge(first_loaded, 16)

            def turn(t):
                for hf in range(2):
                    for m in range(UNITS):
                        s = m - CHAIN_AT
                        if m == 0 and t.has(hf):
                            c = t.chunk(hf)
                            pe.wait_ge(x_loaded[hf], 16 * (t.i + 1))
                            wait(pe, h_ready, STEPS * c)
                            project(ps_rnn, wx, x_in[hf])
                        if m == 0 and t.has(hf - 1):
                            c = t.chunk(hf - 1)
                            if t.at(0):
                                pe.wait_ge(prep, PREP_OPS)
                            pe.wait_ge(x1_done, c + 1)
                            wait(pe, membrane, STEPS * c)
                            project(ps_spike, w_spike, x1[1 - hf])
                        if m == 0 and t.has(hf - 2):
                            c = t.chunk(hf - 2)
                            pe.wait_ge(x2_done, c + 1)
                            wait(pe, gate_ops, GATE_OPS * (c - 1) + 1)
                            if hf == 1 and t.has_pair(-3):
                                pe.wait_ge(out_done, KD * t.chunk(-4))
                            for q in range(QB):
                                last = products(ps_misc[:, 0, q * N_ROUTED:(q + 1) * N_ROUTED],
                                                [(x2[hf][:, k, q * P:(q + 1) * P], router[:, k, :]) for k in range(KD)], first=q == 0)
                            last.then_inc(router_sums, 1)
                        if 0 <= s < STEPS and t.has(hf):
                            c = t.chunk(hf)
                            if t.at(0) and hf == 0 and s == 0:
                                pe.wait_ge(h_start, 1)
                            wait(pe, h_ready, STEPS * c + s)
                            for mt in range(KD):
                                last = products(ps_rnn[:, mt, cols[s]], [(wh[:, k, mt * P:(mt + 1) * P], h_rnn[hf][:, k, cols[s]]) for k in range(KD)], first=False)
                            last.then_inc(rnn_sums, 1)
                        if 0 <= s < STEPS and t.has(hf - 1):
                            c = t.chunk(hf - 1)
                            if t.at(0) and hf == 1 and s == 0:
                                pairs = [(v, cnd) for v, cnd in ((v_hi, cond_hi), (v_hi, cond_lo), (v_lo, cond_hi))]
                                sl = slice(0, B)
                            else:
                                wait(pe, spiked, STEPS * c + s)
                                before = spikes[1 - hf] if s else spikes[hf]
                                sl = cols[s - 1]
                                pairs = [(v_hi, before), (v_lo, before)]
                            for mt in range(KD):
                                last = products(ps_spike[:, mt, cols[s]], [(v[:, k, mt * P:(mt + 1) * P], d[:, k, sl]) for k in range(KD) for v, d in pairs], first=False)
                            last.then_inc(spike_sums, 1)
                        if t.has(hf - 2):
                            c = t.chunk(hf - 2)
                            if m == 0:
                                if t.at(1) and hf == 0:
                                    pe.wait_ge(stage_lo, STAGES)
                                pe.wait_ge(x2_lo_done, c + 1)
                            unit_hidden(c, m, hf)
                        if m >= LAG and t.has(hf - 2):
                            unit_output(t.chunk(hf - 2), m - LAG)
                        if m < LAG and t.has(hf - 3):
                            unit_output(t.chunk(hf - 3), UNITS + m - LAG)
                        if hf == 0 and t.has_pair(-3):
                            j = t.i - 3
                            if m in (1, 3):
                                q = m // 2
                                if q == 0:
                                    pe.wait_ge(taps_done, TAP_OPS * (j + 1))
                                    if t.has(-2):
                                        pe.wait_ge(gate_ops, GATE_OPS * t.chunk(-2) + 1)
                                    else:
                                        pe.wait_ge(gate_ops, GATE_OPS * CHUNKS)
                                    wait(pe, out_done, KD * 2 * j)
                                else:
                                    pe.wait_ge(post_copied, 3 * (2 * j + 1))
                                products(ps_misc[:, 0, :], [(proj[:, k, :], conv[:, k, halves[q]]) for k in range(KD)])
                                products(ps_misc[0:N_STATE, 1, :], [(skip[:, k, :], hist[:, k, HIST + q * TOK:HIST + (q + 1) * TOK]) for k in range(KD)], first=False).then_inc(post_sums, 1)
                            if m in (6, 8):
                                q = (m - 6) // 2
                                if q == 0:
                                    pe.wait_ge(post_copied, 3 * (2 * j + 2))
                                    pe.wait_ge(post_ops, POST_OPS * (j + 1))
                                else:
                                    pe.wait_ge(out_done, KD * (2 * j + 1))
                                for mt in range(KD):
                                    last = products(ps_misc[:, mt, :], [(w_out_dt[:, mt * P:(mt + 1) * P], y_t[:, halves[q]])], first=mt == 0)
                                last.then_inc(out_sums, 1)

            run_turns(pe, turn)

        @block.scalar
        def _(act):
            nc.scalar.preload_act_table_set("natural_log_exp_and_others")
            act.wait_ge(small_loaded, 16)
            lg = logs[0:N_STATE, :]
            nc.scalar.activation(state_abs[:], lg, ACT.Abs).then_inc(prep_act, 1)
            act.wait_ge(prep_act, 1)
            nc.scalar.activation(state_exp[:], state_abs[:], ACT.Exp, scale=-1.0).then_inc(prep_act, 1)
            act.wait_ge(prep_act, 2)
            nc.scalar.activation(state_ln[:], state_exp[:], ACT.Ln, bias=1.0).then_inc(prep_act, 1)
            nc.scalar.preload_act_table_set("gelu_and_others")

            def weight_stage(j):
                act.wait_ge(stage_loaded[j % 2], 16 * (j // 2 + 1))
                nc.scalar.activation(w_hi[:, j * STAGE:(j + 1) * STAGE], stage[:, j % 2, :], ACT.Copy, scale=W_SCALE).then_inc(stage_hi, 1)

            def turn(t):
                for hf in range(2):
                    for m in range(UNITS):
                        s = m - CHAIN_AT
                        if t.at(0) and (UNITS * hf + m) % 3 == 1 and (UNITS * hf + m) // 3 < STAGES:
                            weight_stage((UNITS * hf + m) // 3)
                        if 0 <= s < STEPS and t.has(hf):
                            c = t.chunk(hf)
                            act.wait_ge(rnn_sums, STEPS * c + s + 1)
                            if s == STEPS - 1:
                                wait(act, x1_done, c)
                                dst = h_rnn[1 - hf][:, :, cols[0]]
                            else:
                                dst = h_rnn[hf][:, :, cols[s + 1]]
                            nc.scalar.activation(dst, ps_rnn[:, :, cols[s]], ACT.Tanh).then_inc(h_ready, 1)
                        if t.has(hf - 2):
                            c = t.chunk(hf - 2)
                            if m == 0:
                                act.wait_ge(gate_ops, GATE_OPS * c + 1)
                                nc.scalar.activation(half_scores[:], logits[:], ACT.Tanh, scale=0.5).then_inc(scored, 1)
                            act.wait_ge(hidden, UNITS * c + m + 1)
                            if m < SHARED_UNITS:
                                wait(act, evacuated, SHARED_UNITS * c + m - 1)
                                nc.scalar.activation(act_f[m % 2][:], ps_hid[(2 * m) % BANKS][:], ACT.Tanh, scale=0.5 / W_SCALE).then_inc(activated, 1)
                            else:
                                act.wait_ge(lo_done, UNITS * c + m - 1)
                                nc.scalar.activation(hid[m % 2][:], ps_hid[(SHARED_UNITS + m) % BANKS][:], ACT.Gelu, scale=1.0 / W_SCALE).then_inc(activated, 1)
                        if m >= 1 and t.has(hf - 2) or m == 0 and t.has(hf - 3):
                            c = t.chunk(hf - 2) if m else t.chunk(hf - 3)
                            n = (m - 1) % UNITS
                            if n < SHARED_UNITS:
                                act.wait_ge(evacuated, SHARED_UNITS * c + n + 1)
                            else:
                                act.wait_ge(gated, N_ROUTED * c + n - SHARED_UNITS + 1)
                            wait(act, summed, UNITS * c + n - 3)
                            nc.scalar.activation(hid_hi[n % 4][:], hid[n % 2][:], ACT.Copy).then_inc(hi_done, 1)
                        if m == UNITS - 1 and t.has(hf - 1):
                            c = t.chunk(hf - 1)
                            act.wait_ge(x2_done, c + 1)
                            wait(act, hidden, UNITS * (c - 1))
                            nc.scalar.activation(x2_hi[1 - hf][:], x2[1 - hf][:], ACT.Copy).then_inc(x2_hi_done, 1)
                        if hf == 0 and t.has_pair(-3):
                            j = t.i - 3
                            if m in (1, 3):
                                q = m // 2
                                act.wait_ge(post_sums, 2 * j + q + 1)
                                if q == 0:
                                    wait(act, post_ops, POST_OPS * j)
                                nc.scalar.activation(z_b[:, halves[q]], ps_misc[0:N_STATE, 0, :], ACT.Identity, bias=proj_bias[0:N_STATE, :]).then_inc(post_copied, 1)
                                nc.scalar.activation(c_t[:, halves[q]], ps_misc[N_STATE:P, 0, :], ACT.Tanh, bias=proj_bias[N_STATE:P, :]).then_inc(post_copied, 1)
                                nc.scalar.activation(u_t[:, halves[q]], ps_misc[0:N_STATE, 1, :], ACT.Identity, bias=skip_bias[0:N_STATE, :]).then_inc(post_copied, 1)
                            if m == 4:
                                act.wait_ge(post_copied, 3 * (2 * j + 2))
                                nc.scalar.activation(z_abs[:], z_b[:], ACT.Abs).then_inc(post_act, 1)
                                nc.scalar.preload_act_table_set("natural_log_exp_and_others")
                                act.wait_ge(post_act, 3 * j + 1)
                                nc.scalar.activation(z_exp[:], z_abs[:], ACT.Exp, scale=-1.0).then_inc(post_act, 1)
                                act.wait_ge(post_act, 3 * j + 2)
                                nc.scalar.activation(z_ln[:], z_exp[:], ACT.Ln, bias=1.0).then_inc(post_act, 1)
                                nc.scalar.preload_act_table_set("gelu_and_others")

            run_turns(act, turn)

        @block.vector
        def _(dve):
            n_prep = [0]

            def prepared(ins):
                n_prep[0] += 1
                ins.then_inc(prep, 1)
                dve.wait_ge(prep, n_prep[0])

            dve.wait_ge(first_loaded, 16)
            nc.vector.tensor_copy(h_rnn[0][:, :, cols[0]], cond).then_inc(h_start, 1)
            dve.wait_ge(small_loaded, 16)
            prepared(nc.vector.tensor_scalar(neg_a[:], alpha_col, A_LO, A_HI, ALU.max, ALU.min))
            prepared(nc.vector.tensor_scalar(neg_a[:], neg_a[:], -1.0, None, ALU.mult))
            prepared(nc.vector.tensor_scalar(keep_row[:], alpha_row, A_LO, A_HI, ALU.max, ALU.min))
            prepared(nc.vector.tensor_scalar(keep_row[:], keep_row[:], -W_SCALE, W_SCALE, ALU.mult, ALU.add))
            keep2 = keep_row[:].rearrange("p (k n) -> p k n", k=1).broadcast_to((P, KD, D))
            prepared(nc.vector.tensor_tensor(w_spike[:], w_in, keep2, ALU.mult))
            prepared(nc.vector.tensor_tensor(v_in, v_in, off_diag, ALU.mult))
            prepared(nc.vector.tensor_tensor(v_in, v_in, keep2, ALU.mult))
            prepared(nc.vector.tensor_copy(v_hi[:], v_in))
            prepared(nc.vector.tensor_tensor(v_lo[:], v_in, v_hi[:], ALU.subtract))
            prepared(nc.vector.tensor_copy(cond_hi[:], cond))
            prepared(nc.vector.tensor_tensor(cond_lo[:], cond, cond_hi[:], ALU.subtract))
            prepared(nc.vector.memset(leak[:], 0.0))
            dve.wait_ge(cond_mm, 1)
            prepared(nc.vector.tensor_copy(cond_logits[:], ps_misc[:, 0, 0:N_ROUTED]))
            dve.wait_ge(prep_act, 3)
            prepared(nc.vector.scalar_tensor_tensor(state_sp[:], logs[0:N_STATE, :], 0.0, state_ln[:], ALU.max, ALU.add))
            prepared(nc.vector.tensor_tensor(step_a[:], state_sp[:, 0:1], state_sp[:, 1:2], ALU.mult))
            assert n_prep[0] == PREP_OPS
            prepared(nc.vector.tensor_scalar(decay[:], step_a[:], -1.0, 1.0, ALU.mult, ALU.add))
            prepared(nc.vector.memset(decay_run[:], 1.0))
            prepared(nc.vector.tensor_scalar(decay_run[:], decay_run[:], decay[:, 0:1], None, ALU.mult))
            prepared(nc.vector.memset(decay_run[:, :, 0:1], 0.0))
            prepared(nc.vector.tensor_scalar(w_out_dt[:], w_out[0:N_STATE, :], state_sp[:, 1:2], None, ALU.mult))
            prepared(nc.vector.memset(state[:], 0.0))

            def weight_stage(j):
                dve.wait_ge(stage_hi, j + 1)
                nc.vector.scalar_tensor_tensor(w_lo[:, j * STAGE:(j + 1) * STAGE], stage[:, j % 2, :], W_SCALE,
                                               w_hi[:, j * STAGE:(j + 1) * STAGE], ALU.mult, ALU.subtract).then_inc(stage_lo, 1)

            def spike_step(c, s, par):
                dve.wait_ge(spike_sums, STEPS * c + s + 1)
                wait(dve, leak_done, STEPS * c + s)
                nc.vector.scalar_tensor_tensor(u_mem[:], ps_spike[:, :, cols[s]], 1.0 / W_SCALE, leak[:], ALU.mult, ALU.add).then_inc(membrane, 1)
                if s == 0:
                    wait(dve, x2_done, c - 1)
                dve.wait_ge(membrane, STEPS * c + s + 1)
                nc.vector.tensor_scalar(spikes[par][:, :, cols[s]], u_mem[:], 1.0, None, ALU.is_gt).then_inc(spiked, 1)
                nc.vector.scalar_tensor_tensor(excess[:], u_mem[:], 1.0, u_mem[:], ALU.is_gt, ALU.subtract).then_inc(excess_done, 1)
                dve.wait_ge(excess_done, STEPS * c + s + 1)
                nc.vector.tensor_tensor(leak[:], excess[:], neg_a[:], ALU.mult).then_inc(leak_done, 1)

            def unit_evacuate(c, m):
                dve.wait_ge(activated, UNITS * c + m + 1)
                nc.vector.scalar_tensor_tensor(silu[m % 2][:], act_f[m % 2][:], 1.0, ps_hid[(2 * m) % BANKS][:], ALU.add, ALU.mult).then_inc(silu_done, 1)
                dve.wait_ge(silu_done, SHARED_UNITS * c + m + 1)
                nc.vector.scalar_tensor_tensor(hid[m % 2][:], ps_hid[(2 * m + 1) % BANKS][:], H_SCALE / (2.0 * N_SHARED * LAYER * W_SCALE * W_SCALE),
                                               silu[m % 2][:], ALU.mult, ALU.mult).then_inc(evacuated, 1)

            def gate_steps(c, par):
                done = [1]

                def step(ins):
                    done[0] += 1
                    ins.then_inc(gate_ops, 1)

                def settle():
                    dve.wait_ge(gate_ops, GATE_OPS * c + done[0])

                def hold():
                    nc.vector.memset(dve_hold[:], 0.0)

                dve.wait_ge(scored, c + 1)
                step(nc.vector.tensor_scalar(scores[:], half_scores[:], 0.5, 0.5, ALU.mult, ALU.add))
                settle()
                step(nc.vector.tensor_tensor(select[:], scores[:], router_bias, ALU.add))
                settle()
                hold()
                for q in range(QB):
                    step(nc.vector.max(top[:, q, :], select[:, q, :]))
                settle()
                hold()
                for q in range(QB):
                    step(nc.vector.max_index(top_at[:, q, :], top[:, q, :], select[:, q, :]))
                settle()
                step(nc.vector.tensor_copy(top_at_f[:], top_at[:, :, 0:2]))
                settle()
                for q in range(QB):
                    step(nc.vector.tensor_scalar(chosen0[:, q, :], iota, top_at_f[:, q, 0:1], None, ALU.is_equal))
                settle()
                for q in range(QB):
                    step(nc.vector.scalar_tensor_tensor(chosen[:, q, :], iota, top_at_f[:, q, 1:2], chosen0[:, q, :], ALU.is_equal, ALU.add))
                settle()
                step(nc.vector.tensor_tensor(picked[:], chosen[:], scores[:], ALU.mult))
                settle()
                step(nc.vector.tensor_reduce(denom[:], picked[:], AX_X, ALU.add))
                settle()
                step(nc.vector.tensor_scalar(denom_eps[:], denom[:], 1e-9, None, ALU.add))
                step(nc.vector.tensor_scalar(denom_ok[:], denom[:], 1e-9, None, ALU.is_gt))
                settle()
                unit = H_SCALE / LAYER
                step(nc.vector.reciprocal(denom_inv[:], denom_eps[:]))
                step(nc.vector.tensor_scalar(gate_even[:], denom_ok[:], -0.5 * unit, 0.5 * unit, ALU.mult, ALU.add))
                settle()
                step(nc.vector.scalar_tensor_tensor(gate_scale[:], denom_inv[:], unit, denom_ok[:], ALU.mult, ALU.mult))
                settle()
                for q in range(QB):
                    step(nc.vector.tensor_scalar(gate_a[:, q, :], scores[:, q, :], gate_scale[:, q:q + 1], gate_even[:, q:q + 1], ALU.mult, ALU.add))
                settle()
                wait(dve, gates_stored, 16 * (c - 1))
                step(nc.vector.tensor_tensor(gates[par][:], gate_a[:], chosen[:], ALU.mult))
                assert done[0] == GATE_OPS, done[0]

            def tap(j, n):
                k, kd = n // KD, n % KD
                window = hist[:, kd, k * B:k * B + PAIR]
                if k == 0:
                    if kd == 0:
                        dve.wait_ge(hist_ready, j + 1)
                        wait(dve, post_sums, 2 * j)
                    ins = nc.vector.tensor_scalar(conv[:, kd, :], window, cond[:, kd, 0:1], conv_bias[:, kd:kd + 1], ALU.mult, ALU.add)
                else:
                    dve.wait_ge(taps_done, TAP_OPS * j + n - KD + 1)
                    ins = nc.vector.scalar_tensor_tensor(conv[:, kd, :], window, cond[:, kd, k:k + 1], conv[:, kd, :], ALU.mult, ALU.add)
                ins.then_inc(taps_done, 1)

            def scan(j):
                by_time = lambda ap: ap.rearrange("p (t b) -> p t b", b=B)
                turned = lambda ap: ap[:].rearrange("p b t -> p t b")
                dve.wait_ge(post_act, 3 * (j + 1))
                nc.vector.scalar_tensor_tensor(b_t[:], z_b[:], 0.0, z_ln[:], ALU.max, ALU.add).then_inc(post_ops, 1)
                dve.wait_ge(post_ops, POST_OPS * j + 1)
                nc.vector.tensor_tensor(turned(drive), by_time(b_t[:]), by_time(u_t[:]), ALU.mult).then_inc(post_ops, 1)
                dve.wait_ge(post_ops, POST_OPS * j + 2)
                nc.vector.scalar_tensor_tensor(drive[:, :, 0], state[:, :, 2 * STEPS - 1], decay[:, 0:1], drive[:, :, 0], ALU.mult, ALU.add).then_inc(post_ops, 1)
                dve.wait_ge(post_ops, POST_OPS * j + 3)
                nc.vector.tensor_tensor_scan(state[:].rearrange("p b t -> p (b t)"), decay_run[:].rearrange("p b t -> p (b t)"),
                                             drive[:].rearrange("p b t -> p (b t)"), 0.0, ALU.mult, ALU.add).then_inc(post_ops, 1)
                dve.wait_ge(post_ops, POST_OPS * j + 4)
                wait(dve, out_sums, 2 * j)
                nc.vector.tensor_tensor(by_time(y_t[:]), by_time(c_t[:]), turned(state), ALU.mult).then_inc(post_ops, 1)

            def turn(t):
                for hf in range(2):
                    for m in range(UNITS):
                        s = m - CHAIN_AT
                        if t.at(0) and (UNITS * hf + m) % 3 == 1 and (UNITS * hf + m) // 3 < STAGES:
                            weight_stage((UNITS * hf + m) // 3)
                        if m == 0 and t.has(hf - 2):
                            c = t.chunk(hf - 2)
                            dve.wait_ge(router_sums, c + 1)
                            wait(dve, scored, c)
                            nc.vector.tensor_tensor(logits[:], ps_misc[:, 0, 0:QB * N_ROUTED].rearrange("p (q e) -> p q e", q=QB),
                                                    cond_logits[:].rearrange("p (q e) -> p q e", q=1).broadcast_to((P, QB, N_ROUTED)), ALU.add).then_inc(gate_ops, 1)
                        if m == LAG and t.has(hf - 3):
                            c = t.chunk(hf - 3)
                            dve.wait_ge(summed, UNITS * (c + 1))
                            wait(dve, hist_ready, t.i - 2 + hf)
                            nc.vector.scalar_tensor_tensor(x3_new[:, :, halves[1 - hf]], ps_y[:], Y_SCALE, x2[1 - hf][:], ALU.mult, ALU.add).then_inc(x3_done, 1)
                        if 0 <= s < STEPS and t.has(hf - 1):
                            spike_step(t.chunk(hf - 1), s, 1 - hf)
                        if m < SHARED_UNITS and t.has(hf - 2):
                            unit_evacuate(t.chunk(hf - 2), m)
                        if m == 0 and t.has(hf - 2):
                            gate_steps(t.chunk(hf - 2), hf)
                        todo = list(taps_at(UNITS * hf + m)) if t.has_pair(-2) else []
                        for n in todo[:len(todo) // 2]:
                            tap(t.i - 2, n)
                        if m >= 1 and t.has(hf - 2) or m == 0 and t.has(hf - 3):
                            c = t.chunk(hf - 2) if m else t.chunk(hf - 3)
                            n = (m - 1) % UNITS
                            dve.wait_ge(hi_done, UNITS * c + n + 1)
                            nc.vector.tensor_tensor(hid_lo[n % 4][:], hid[n % 2][:], hid_hi[n % 4][:], ALU.subtract).then_inc(lo_done, 1)
                        for n in todo[len(todo) // 2:]:
                            tap(t.i - 2, n)
                        if hf == 0 and t.has_pair(-3):
                            j = t.i - 3
                            if m == 5:
                                scan(j)
                            if m in (7, 9):
                                q = (m - 7) // 2
                                dve.wait_ge(out_sums, 2 * j + q + 1)
                                wait(dve, out_stored, 16 * (2 * j))
                                shifted = HIST
                                if t.has_pair(-2):
                                    dve.wait_ge(hist_ready, j + 2)
                                    shifted = HIST - PAIR
                                for kd in range(KD):
                                    nc.vector.scalar_tensor_tensor(out_sb[q][:, kd, :], ps_misc[:, kd, :], out_bias[:, kd:kd + 1],
                                                                   hist[:, kd, shifted + q * TOK:shifted + (q + 1) * TOK], ALU.add, ALU.add).then_inc(out_done, 1)

            run_turns(dve, turn)

        @block.gpsimd
        def _(pool):
            nc.gpsimd.memset(pool_hold[:], 0.0).then_inc(pool_start, 1)
            nc.gpsimd.memset(hist[:], 0.0).then_inc(pool_start, 1)
            pool.wait_ge(pool_start, 2)

            def hold():
                nc.gpsimd.tensor_tensor(pool_hold[:], pool_hold[:], pool_hold[:], ALU.mult)

            def turn(t):
                for hf in range(2):
                    for m in range(UNITS):
                        if m >= SHARED_UNITS and t.has(hf - 2):
                            c = t.chunk(hf - 2)
                            e = m - SHARED_UNITS
                            if e == 0:
                                pool.wait_ge(gates_loaded[hf], 16 * t.i)
                            pool.wait_ge(activated, UNITS * c + m + 1)
                            gate = gates_all[hf][:, :, e:e + 1].rearrange("p n o -> p o n").broadcast_to((P, 2, TOK))
                            nc.gpsimd.tensor_tensor(hid[m % 2][:], hid[m % 2][:], gate, ALU.mult).then_inc(gated, 1)
                        if hf == 0 and m == 4 and t.has_pair(-2):
                            j = t.i - 2
                            pool.wait_ge(x3_done, 2 * (j + 1))
                            wait(pool, taps_done, TAP_OPS * j)
                            wait(pool, post_sums, 2 * j)
                            wait(pool, out_done, KD * 2 * (j - 1))
                            at = HIST // 2
                            hold()
                            nc.gpsimd.tensor_copy(hist[:, :, 0:at], hist[:, :, PAIR:PAIR + at]).then_inc(hist_half, 1)
                            pool.wait_ge(hist_half, 2 * j + 1)
                            hold()
                            nc.gpsimd.tensor_copy(hist[:, :, at:HIST], hist[:, :, PAIR + at:PAIR + HIST]).then_inc(hist_half, 1)
                            pool.wait_ge(hist_half, 2 * j + 2)
                            hold()
                            nc.gpsimd.tensor_copy(hist[:, :, HIST:], x3_new[:]).then_inc(hist_ready, 1)
                        if m == 9 and t.has(hf):
                            c = t.chunk(hf)
                            pool.wait_ge(h_ready, STEPS * c + STEPS - 1)
                            pool.wait_ge(x_loaded[hf], 16 * (t.i + 1))
                            wait(pool, x2_done, c - 1)
                            nc.gpsimd.tensor_tensor(x1[hf][:], x_in[hf][:], h_rnn[hf][:], ALU.add).then_inc(x1_done, 1)
                        if m == 10 and t.has(hf - 1):
                            c = t.chunk(hf - 1)
                            pool.wait_ge(spiked, STEPS * (c + 1))
                            wait(pool, x3_done, c - 1)
                            nc.gpsimd.tensor_tensor(x2[1 - hf][:], x1[1 - hf][:], spikes[1 - hf][:], ALU.add).then_inc(x2_done, 1)
                        if m == 11 and t.has(hf - 1):
                            c = t.chunk(hf - 1)
                            pool.wait_ge(x2_hi_done, c + 1)
                            nc.gpsimd.tensor_tensor(x2_lo[1 - hf][:], x2[1 - hf][:], x2_hi[1 - hf][:], ALU.subtract).then_inc(x2_lo_done, 1)

            run_turns(pool, turn)


def kernel(**inputs):
    import numpy as np
    import concourse.bacc as bacc
    from concourse.bass_utils import run_bass_kernel_spmd

    a = {k: np.asarray(v) for k, v in inputs.items()}

    def rows(w):
        n = w.shape[1]
        return w.reshape(-1, P, n).transpose(1, 0, 2).reshape(P, -1)

    def lay(v, width):
        full = np.zeros((P, width), np.float32)
        full[:v.shape[0], :v.shape[1]] = v
        return full

    c = a["cond_1024"]
    everywhere = lambda v: np.broadcast_to(v[None, :], (P, v.shape[0]))
    column = lambda v: v.reshape(-1, 1)
    alpha = a["L1_cond_alpha"]
    parts = {
        "wx": rows(a["L0_cond_Wx"].T), "wh": rows(a["L0_cond_Wh"].T), "cond": rows(c.T),
        "alpha_col": rows(np.broadcast_to(alpha[:, None], (D, B))),
        "w": rows(a["L1_cond_W"].T), "v": rows(a["L1_cond_V"]),
        "off_diag": rows(1.0 - np.eye(D, dtype=np.float32)), "alpha_row": everywhere(alpha),
        "cond4": rows(np.tile(c.T, (1, P // B))), "router": rows(a["L2_cond_W_router"].T),
        "router_bias": everywhere(np.tile(a["L2_cond_router_bias"], QB)),
        "iota": everywhere(np.arange(N_ROUTED, dtype=np.float32)),
        "proj": rows(a["L3_cond_Wp"]), "skip": rows(a["L3_cond_Ws"]), "out": lay(a["L3_cond_Wo"], D),
        "proj_bias": column(a["L3_cond_bp"]), "skip_bias": lay(column(a["L3_cond_bs"]), 1),
        "out_bias": rows(column(a["L3_cond_bo"])), "conv_bias": rows(column(a["L3_cond_conv_b"])),
        "logs": lay(np.stack([a["L3_cond_A_log"], a["L3_cond_dt_log"]], 1), 2),
    }
    small = np.ascontiguousarray(np.concatenate([parts[n] for n, _ in _SMALL], 1))
    experts = lambda w: np.concatenate([rows(w[e].T) for e in range(w.shape[0])], 1)
    big = np.ascontiguousarray(np.concatenate(
        [experts(a[f"L2_cond_{n}"]) for n in ("s_w1", "s_w3", "s_w2", "r_w1", "r_w2")], 1))
    x = np.ascontiguousarray(a["x"].transpose(2, 1, 0).reshape(KD, P, T * B).transpose(1, 0, 2))

    nc = bacc.Bacc("TRN2", target_bir_lowering=False, num_devices=1)
    arrays = {"x_t": x, "small_w": small, "big_w": big}
    args = [nc.dram_tensor(n, v.shape, F32, kind="ExternalInput").ap() for n, v in arrays.items()]
    args.append(nc.dram_tensor("out_t", (P, KD, T * B), F32, kind="ExternalOutput").ap())
    args.append(nc.dram_tensor("gates_scratch", (2, TOK, N_ROUTED), F32, kind="Internal").ap())
    build(nc, *args)
    r = run_bass_kernel_spmd(nc, [arrays], core_ids=[0])
    y = r.results[0]["out_t"]
    return np.ascontiguousarray(y.transpose(1, 0, 2).reshape(D, T, B).transpose(2, 1, 0))
```

```python
from contextlib import ExitStack

import concourse.bass as bass
from concourse import mybir

ALU = mybir.AluOpType
ACT = mybir.ActivationFunctionType
AX_X = mybir.AxisListType.X
F32 = mybir.dt.float32
F16 = mybir.dt.float16
U32 = mybir.dt.uint32

P = 128
B, T, D = 32, 256, 256
KD = D // P
N_SHARED, FF_SHARED = 2, 512
N_ROUTED, FF_ROUTED = 8, 256
N_STATE = 64
TAPS = B

STEPS = 8
TOK = STEPS * B
CHUNKS = T // STEPS
PAIRS = CHUNKS // 2
PAIR = 2 * TOK
HIST = (TAPS - 1) * B
QB = TOK // P

SHARED_UNITS = N_SHARED * FF_SHARED // (2 * P)
UNITS = SHARED_UNITS + N_ROUTED
BANKS = 4
LAG = 4
CHAIN_AT = 1

W_SCALE = 64.0
H_SCALE = 16.0
Y_SCALE = 1.0 / (W_SCALE * H_SCALE)
LAYER = 4.0

HIDS = 3
SPLITS = 6

GATE_OPS, CHOICE_OPS = 22, 12
TAP_OPS = KD * TAPS
POST_OPS = 5

_SMALL = [
    ("wx", KD * D), ("wh", KD * D), ("cond", KD * B), ("alpha_col", KD * B),
    ("w", KD * D), ("v", KD * D), ("off_diag", KD * D), ("alpha_row", D),
    ("cond4", KD * P), ("router", 2 * KD * N_ROUTED), ("router_bias", QB * N_ROUTED),
    ("iota", N_ROUTED), ("proj", KD * 2 * N_STATE), ("skip", KD * N_STATE), ("out", D),
    ("proj_bias", 1), ("skip_bias", 1), ("out_bias", KD), ("conv_bias", KD),
    ("logs", 2),
]
SMALL = {}
_at = 0
for _n, _w in _SMALL:
    SMALL[_n] = (_at, _w)
    _at += _w
SMALL_COLS = _at
FIRST_COLS = SMALL["w"][0]

SW1, SW3, SW2 = 0, 2048, 4096
RW1 = 6144
RW2 = RW1 + N_ROUTED * KD * FF_ROUTED
BIG_COLS = RW2 + N_ROUTED * KD * FF_ROUTED
STAGE = 2048
STAGES = BIG_COLS // STAGE

A_LO = 0.8187307530779818
A_HI = 0.9607894391523232


def last_user(m):
    use = lambda j: 2 * j + 1 if j < SHARED_UNITS else SHARED_UNITS + j
    before = use(m) - BANKS
    if before < 0:
        before += 2 * SHARED_UNITS + N_ROUTED
        return (before // 2 if before < 2 * SHARED_UNITS else before - SHARED_UNITS) - UNITS
    return before // 2 if before < 2 * SHARED_UNITS else before - SHARED_UNITS


_TAPS = [0, 0, 0, 0, 0, 0, 0, 3, 3, 3, 3, 3,
         4, 3, 3, 3, 3, 3, 3, 3, 3, 3, 3, 3,
         4, 2, 3, 3]

assert sum(_TAPS) == TAP_OPS and len(_TAPS) <= 2 * UNITS + LAG


def taps_at(slot):
    done = sum(_TAPS[:slot])
    return range(done, done + (_TAPS[slot] if slot < len(_TAPS) else 0))


class Turn:

    def __init__(self, i):
        self.i = i

    def chunk(self, offset):
        return self.i * 2 + offset

    def has(self, offset):
        return not isinstance(self.i, int) or 0 <= 2 * self.i + offset < CHUNKS

    def at(self, i):
        return isinstance(self.i, int) and self.i == i

    def has_pair(self, offset):
        return not isinstance(self.i, int) or 0 <= self.i + offset < PAIRS


X2_AT = 8
X1_AT = 9
SCAN_AT = 3
SHIFT_AT = (4, 5, 6)
FIRST_TURN, LAST_TURN = 4, PAIRS - 1
TURNS = PAIRS + 3


def run_turns(engine, body, first=FIRST_TURN, last=LAST_TURN):
    for i in range(first):
        body(Turn(i))
    with engine.Fori(first, last + 1) as i:
        body(Turn(i))
    for i in range(last + 1, TURNS):
        body(Turn(i))


def wait(engine, sem, value):
    if not isinstance(value, int) or value > 0:
        engine.wait_ge(sem, value)


def build(nc: bass.Bass, x_t: bass.AP, small_w: bass.AP, big_w: bass.AP, out_t: bass.AP, gates_dram: bass.AP):
    with ExitStack() as ctx:
        def sb(name, shape, dt=F32):
            return ctx.enter_context(nc.sbuf_tensor(name, shape, dt))

        def psum(name, shape):
            return ctx.enter_context(nc.psum_tensor(name, shape, F32))

        def sem(name):
            return ctx.enter_context(nc.semaphore(name))

        small = sb("small", [P, SMALL_COLS])

        def part(name, **axes):
            at, w = SMALL[name]
            ap = small[:, at:at + w]
            if not axes:
                return ap
            names = " ".join(axes)
            first = next(iter(axes))
            return ap.rearrange(f"p ({names}) -> p {names}", **{first: axes[first]})

        wx, wh = part("wx", k=KD, n=D), part("wh", k=KD, n=D)
        cond = part("cond", k=KD, b=B)
        alpha_col = part("alpha_col", k=KD, b=B)
        w_in, v_in, off_diag = part("w", k=KD, n=D), part("v", k=KD, n=D), part("off_diag", k=KD, n=D)
        alpha_row = part("alpha_row")
        cond4 = part("cond4", k=KD, n=P)
        router = part("router", k=2 * KD, e=N_ROUTED)
        router_bias = part("router_bias", q=QB, e=N_ROUTED)
        iota = part("iota")
        proj, skip = part("proj", k=KD, n=2 * N_STATE), part("skip", k=KD, n=N_STATE)
        w_out = part("out")
        proj_bias, skip_bias = part("proj_bias"), part("skip_bias")
        out_bias, conv_bias = part("out_bias"), part("conv_bias")
        logs = part("logs")

        stage = sb("stage", [P, 2, STAGE])
        w_hi = sb("w_hi", [P, BIG_COLS], F16)
        w_lo = sb("w_lo", [P, BIG_COLS], F16)
        wx_split = [sb(f"wx_split{j}", [P, KD, D], F16) for j in range(2)]
        wh_split = [sb(f"wh_split{j}", [P, KD, D], F16) for j in range(2)]
        w_spike = sb("w_spike", [P, KD, D])
        w_spike_split = [sb(f"w_spike_split{j}", [P, KD, D], F16) for j in range(2)]
        router_split = [sb(f"router_split{j}", [P, KD, N_ROUTED], F16) for j in range(2)]
        v_split = [sb(f"v_split{j}", [P, KD, D], F16) for j in range(2)]
        keep_row = sb("keep_row", [P, D])
        a_row = sb("a_row", [P, D])
        on_diag = sb("on_diag", [P, KD, D])
        a_col = sb("a_col", [P, KD])
        cond_split = [sb(f"cond_split{j}", [P, KD, B], F16) for j in range(2)]
        cond_logits = sb("cond_logits", [P, N_ROUTED])
        state_abs = sb("state_abs", [N_STATE, 2])
        state_exp = sb("state_exp", [N_STATE, 2])
        state_ln = sb("state_ln", [N_STATE, 2])
        state_sp = sb("state_sp", [N_STATE, 2])
        step_a = sb("step_a", [N_STATE, 1])
        decay = sb("decay", [N_STATE, 1])
        decay_run = sb("decay_run", [N_STATE, B, 2 * STEPS])
        w_out_dt = sb("w_out_dt", [N_STATE, D])

        x_in = [sb(f"x_in{p}", [P, KD, TOK]) for p in range(2)]
        h_rnn = [sb(f"h_rnn{p}", [P, KD, TOK]) for p in range(2)]
        x_split = [[sb(f"x_split{p}{j}", [P, KD, TOK], F16) for j in range(2)] for p in range(2)]
        h_split = [[sb(f"h_split{p}{j}", [P, KD, TOK], F16) for j in range(2)] for p in range(2)]
        x1_split = [[sb(f"x1_split{p}{j}", [P, KD, TOK], F16) for j in range(2)] for p in range(2)]
        x1 = [sb(f"x1_{p}", [P, KD, TOK]) for p in range(2)]
        u_mem = sb("u_mem", [P, KD, B])
        spikes = [sb(f"spikes{p}", [P, KD, TOK], F16) for p in range(2)]
        x2 = [sb(f"x2_{p}", [P, KD, TOK]) for p in range(2)]
        x2_split = [[sb(f"x2_split{p}{j}", [P, KD, TOK], F16) for j in range(2)] for p in range(2)]
        act_f = [sb(f"act_f{j}", [P, 2, TOK]) for j in range(2)]
        hid = [sb(f"hid{j}", [P, 2, TOK]) for j in range(HIDS)]
        hid_hi = [sb(f"hid_hi{j}", [P, 2, TOK], F16) for j in range(SPLITS)]
        hid_lo = [sb(f"hid_lo{j}", [P, 2, TOK], F16) for j in range(SPLITS)]
        gates = [sb(f"gates{p}", [P, QB, N_ROUTED]) for p in range(2)]
        gates_all = [stage[:, p, :].rearrange("p (n e) -> p n e", e=N_ROUTED) for p in range(2)]
        logits = sb("logits", [P, QB, N_ROUTED])
        half_scores = sb("half_scores", [P, QB, N_ROUTED])
        scores = sb("scores", [P, QB, N_ROUTED])
        select = sb("select", [P, QB, N_ROUTED])
        dve_hold = sb("dve_hold", [P, 1])
        top = sb("top", [P, QB, 8])
        top_at = sb("top_at", [P, QB, 8], U32)
        top_at_f = sb("top_at_f", [P, QB, 2])
        chosen0 = sb("chosen0", [P, QB, N_ROUTED])
        chosen = sb("chosen", [P, QB, N_ROUTED])
        picked = sb("picked", [P, QB, N_ROUTED])
        denom = sb("denom", [P, QB])
        denom_eps = sb("denom_eps", [P, QB])
        denom_inv = sb("denom_inv", [P, QB])
        denom_ok = sb("denom_ok", [P, QB])
        gate_scale = sb("gate_scale", [P, QB])
        gate_even = sb("gate_even", [P, QB])
        gate_a = sb("gate_a", [P, QB, N_ROUTED])
        x3_new = sb("x3_new", [P, KD, PAIR])
        hist = sb("hist", [P, KD, HIST + PAIR])
        conv = sb("conv", [P, KD, PAIR])
        z_b = sb("z_b", [N_STATE, PAIR])
        c_t = sb("c_t", [N_STATE, PAIR])
        u_t = sb("u_t", [N_STATE, PAIR])
        z_abs = sb("z_abs", [N_STATE, PAIR])
        z_exp = sb("z_exp", [N_STATE, PAIR])
        z_ln = sb("z_ln", [N_STATE, PAIR])
        b_t = sb("b_t", [N_STATE, PAIR])
        drive = sb("drive", [N_STATE, B, 2 * STEPS])
        state = sb("state", [N_STATE, B, 2 * STEPS])
        y_t = sb("y_t", [N_STATE, PAIR])
        out_sb = [sb(f"out_sb{q}", [P, KD, TOK]) for q in range(2)]

        ps_rnn = psum("ps_rnn", [P, KD, TOK])
        ps_spike = psum("ps_spike", [P, KD, TOK])
        ps_y = psum("ps_y", [P, KD, TOK])
        ps_misc = psum("ps_misc", [P, KD, TOK])
        ps_hid = [psum(f"ps_hid{j}", [P, 2, TOK]) for j in range(BANKS)]

        first_loaded, small_loaded = sem("first_loaded"), sem("small_loaded")
        stage_loaded = [sem(f"stage_loaded{j}") for j in range(2)]
        stage_hi, stage_lo = sem("stage_hi"), sem("stage_lo")
        rnn_prep, rnn_weights = sem("rnn_prep"), sem("rnn_weights")
        h_start, pool_start = sem("h_start"), sem("pool_start")
        prep, prep_act, cond_mm = sem("prep"), sem("prep_act"), sem("cond_mm")
        x_loaded = [sem(f"x_loaded{p}") for p in range(2)]
        x_hi_done, x_lo_done = sem("x_hi_done"), sem("x_lo_done")
        rnn_sums, h_ready, h_hi_done, h_lo_done = sem("rnn_sums"), sem("h_ready"), sem("h_hi_done"), sem("h_lo_done")
        x1_done, x1_hi_done, x1_lo_done = sem("x1_done"), sem("x1_hi_done"), sem("x1_lo_done")
        spike_sums, membrane, spiked = sem("spike_sums"), sem("membrane"), sem("spiked")
        x2_done, x2_hi_done, x2_lo_done = sem("x2_done"), sem("x2_hi_done"), sem("x2_lo_done")
        router_sums, gate_ops, scored = sem("router_sums"), sem("gate_ops"), sem("scored")
        gates_stored = sem("gates_stored")
        gates_loaded = [sem(f"gates_loaded{p}") for p in range(2)]
        hidden, activated = sem("hidden"), sem("activated")
        evacuated, gated = sem("evacuated"), sem("gated")
        hi_done, lo_done, summed = sem("hi_done"), sem("lo_done"), sem("summed")
        x3_done, hist_moved, hist_ready = sem("x3_done"), sem("hist_moved"), sem("hist_ready")
        taps_done = sem("taps_done")
        post_sums, post_copied, post_act = sem("post_sums"), sem("post_copied"), sem("post_act")
        post_ops, out_sums, out_done = sem("post_ops"), sem("out_sums"), sem("out_done")
        out_stored = sem("out_stored")

        cols = [slice(s * B, (s + 1) * B) for s in range(STEPS)]
        halves = [slice(q * TOK, (q + 1) * TOK) for q in range(2)]
        PREP_OPS = 19
        block = ctx.enter_context(nc.Block())

        @block.sync
        def _(sp):
            sp.dma_start(small[:, 0:FIRST_COLS], small_w[:, 0:FIRST_COLS]).then_inc(first_loaded, 16)
            for c in range(2):
                sp.dma_start(x_in[c][:], x_t[:, :, c * TOK:(c + 1) * TOK]).then_inc(x_loaded[c], 16)
            sp.dma_start(small[:, FIRST_COLS:], small_w[:, FIRST_COLS:]).then_inc(small_loaded, 16)
            for j in range(STAGES):
                if j >= 2:
                    sp.wait_ge(stage_hi, j - 1)
                    sp.wait_ge(stage_lo, j - 1)
                sp.dma_start(stage[:, j % 2, :], big_w[:, j * STAGE:(j + 1) * STAGE]).then_inc(stage_loaded[j % 2], 16)

            def turn(t):
                for hf in range(2):
                    if t.has(hf - 2):
                        c = t.chunk(hf - 2)
                        sp.wait_ge(gate_ops, GATE_OPS * (c + 1))
                        sp.dma_start(gates_dram[hf].rearrange("(q p) e -> p q e", p=P), gates[hf][:]).then_inc(gates_stored, 16)
                        sp.wait_ge(gates_stored, 16 * (c + 1))
                        if t.at(1) and hf == 0:
                            sp.wait_ge(stage_lo, STAGES)
                        wait(sp, gated, N_ROUTED * (c - 1))
                        sp.dma_start(gates_all[hf], gates_dram[hf].rearrange("(o n) e -> o n e", o=1).broadcast_to((P, TOK, N_ROUTED))).then_inc(gates_loaded[hf], 16)
                    if t.has(hf) and t.has(hf + 2):
                        c = t.chunk(hf)
                        sp.wait_ge(x1_done, c + 1)
                        sp.dma_start(x_in[hf][:], x_t[:, :, bass.ds((c + 2) * TOK, TOK)]).then_inc(x_loaded[hf], 16)
                    if hf == 1 and t.has_pair(-3):
                        for q in range(2):
                            n = t.chunk(q - 6)
                            sp.wait_ge(out_done, KD * (n + 1))
                            sp.dma_start(out_t[:, :, bass.ds(n * TOK, TOK)], out_sb[q][:]).then_inc(out_stored, 16)

            run_turns(sp, turn, last=LAST_TURN - 1)
            sp.wait_ge(out_stored, 16 * CHUNKS)

        @block.tensor
        def _(pe):
            PASSES = ((0, 0), (0, 1), (1, 0))

            def products(out, pairs, first=True):
                last = None
                for j, (w, v) in enumerate(pairs):
                    last = nc.tensor.matmul(out, w, v, start=first and j == 0, stop=j == len(pairs) - 1, skip_group_check=True)
                return last

            def project(ps, out_cols, weights, data, data_cols, first):
                passes = PASSES if len(data) == 2 else ((0, 0), (1, 0))
                for mt in range(KD):
                    last = products(ps[:, mt, out_cols], [
                        (weights[a][:, k, mt * P:(mt + 1) * P], data[b][:, k, data_cols])
                        for k in range(KD) for a, b in passes], first=first and mt == 0)
                return last

            def unit_hidden(c, m, par):
                before = last_user(m)
                if before % UNITS < SHARED_UNITS:
                    wait(pe, evacuated, SHARED_UNITS * (c + before // UNITS) + before % UNITS + 1)
                else:
                    wait(pe, activated, UNITS * c + before + 1)
                split = x2_split[par]
                w = (w_hi, w_lo)
                if m < SHARED_UNITS:
                    e, part_ = m // 2, m % 2
                    jobs = [(ps_hid[(2 * m + j) % BANKS], base + e * KD * FF_SHARED + part_ * 2 * P, FF_SHARED)
                            for j, base in enumerate((SW1, SW3))]
                else:
                    e = m - SHARED_UNITS
                    jobs = [(ps_hid[(SHARED_UNITS + m) % BANKS], RW1 + e * KD * FF_ROUTED, FF_ROUTED)]
                for ps, base, ff in jobs:
                    for ft in range(2):
                        last = products(ps[:, ft, :], [
                            (w[a][:, base + k * ff + ft * P:base + k * ff + (ft + 1) * P], split[b][:, k, :])
                            for k in range(KD) for a, b in PASSES], first=ft == 0)
                last.then_inc(hidden, 1)

            def unit_output(c, m):
                pe.wait_ge(lo_done, UNITS * c + m + 1)
                if m == 0:
                    wait(pe, x3_done, c)
                split = (hid_hi[m % SPLITS], hid_lo[m % SPLITS])
                w = (w_hi, w_lo)
                base = SW2 + m * 2 * D if m < SHARED_UNITS else RW2 + (m - SHARED_UNITS) * KD * D
                for mt in range(KD):
                    last = products(ps_y[:, mt, :], [
                        (w[a][:, base + f * D + mt * P:base + f * D + (mt + 1) * P], split[b][:, f, :])
                        for f in range(2) for a, b in PASSES], first=m == 0 and mt == 0)
                last.then_inc(summed, 1)

            pe.wait_ge(small_loaded, 16)
            products(ps_misc[:, 0, 0:N_ROUTED], [(cond4[:, k, :], router[:, KD + k, :]) for k in range(KD)]).then_inc(cond_mm, 1)
            pe.wait_ge(rnn_weights, 1)
            every = slice(0, TOK)

            def turn(t):
                for hf in range(2):
                    for m in range(UNITS):
                        s = m - CHAIN_AT
                        if 0 <= s < STEPS and t.has(hf):
                            c = t.chunk(hf)
                            data, at = (cond_split, slice(0, B)) if t.at(0) and hf == 0 and s == 0 else (h_split[hf], cols[s])
                            wait(pe, h_lo_done, STEPS * c + s)
                            project(ps_rnn, cols[s], wh_split, data, at, first=False).then_inc(rnn_sums, 1)
                        if 0 <= s < STEPS and t.has(hf - 1):
                            c = t.chunk(hf - 1)
                            if t.at(0) and s == 0:
                                data, at = cond_split, slice(0, B)
                            else:
                                wait(pe, spiked, STEPS * c + s)
                                data, at = [spikes[1 - hf] if s else spikes[hf]], cols[s - 1]
                            project(ps_spike, cols[s], v_split, data, at, first=False).then_inc(spike_sums, 1)
                        if t.has(hf - 2):
                            c = t.chunk(hf - 2)
                            if m == 0:
                                if t.at(1) and hf == 0:
                                    pe.wait_ge(stage_lo, STAGES)
                                pe.wait_ge(x2_lo_done, c + 1)
                            unit_hidden(c, m, hf)
                        if m >= LAG and t.has(hf - 2):
                            unit_output(t.chunk(hf - 2), m - LAG)
                        if m < LAG and t.has(hf - 3):
                            unit_output(t.chunk(hf - 3), UNITS + m - LAG)
                        if m == 0 and t.has(hf - 2):
                            c = t.chunk(hf - 2)
                            wait(pe, gate_ops, GATE_OPS * (c - 1) + 1)
                            if hf == 1 and t.has_pair(-3):
                                pe.wait_ge(post_copied, 3 * t.chunk(-4))
                            if hf == 0 and t.has_pair(-4):
                                pe.wait_ge(out_done, KD * t.chunk(-6))
                            for q in range(QB):
                                last = products(ps_misc[:, 0, q * N_ROUTED:(q + 1) * N_ROUTED],
                                                [(x2_split[hf][a][:, k, q * P:(q + 1) * P], router_split[b][:, k, :])
                                                 for k in range(KD) for a, b in PASSES], first=q == 0)
                            last.then_inc(router_sums, 1)
                        if m == 0 and t.has(hf):
                            c = t.chunk(hf)
                            pe.wait_ge(x_lo_done, c + 1)
                            wait(pe, h_ready, STEPS * c)
                            project(ps_rnn, every, wx_split, x_split[hf], every, first=True)
                        if m == 0 and t.has(hf - 1):
                            c = t.chunk(hf - 1)
                            if t.at(0):
                                pe.wait_ge(prep, PREP_OPS)
                            pe.wait_ge(x1_lo_done, c + 1)
                            wait(pe, spiked, STEPS * c)
                            project(ps_spike, every, w_spike_split, x1_split[1 - hf], every, first=True)
                        if hf == 0 and m in (4, 5) and t.has_pair(-3):
                            j, q = t.i - 3, m - 4
                            if q == 0:
                                pe.wait_ge(taps_done, TAP_OPS * (j + 1))
                                pe.wait_ge(gate_ops, GATE_OPS * t.chunk(-2) + 1 if t.has(-2) else GATE_OPS * CHUNKS)
                                wait(pe, out_done, KD * 2 * j)
                            else:
                                pe.wait_ge(post_copied, 3 * (2 * j + 1))
                            products(ps_misc[:, 0, :], [(proj[:, k, :], conv[:, k, halves[q]]) for k in range(KD)])
                            products(ps_misc[0:N_STATE, 1, :], [(skip[:, k, :], hist[:, k, HIST + q * TOK:HIST + (q + 1) * TOK]) for k in range(KD)], first=False).then_inc(post_sums, 1)
                        if hf == 1 and m in (4, 6) and t.has_pair(-3):
                            j, q = t.i - 3, (m - 4) // 2
                            if q == 0:
                                pe.wait_ge(post_copied, 3 * (2 * j + 2))
                                if t.has(-1):
                                    pe.wait_ge(gate_ops, GATE_OPS * t.chunk(-1) + 1)
                                pe.wait_ge(post_ops, POST_OPS * (j + 1))
                            else:
                                pe.wait_ge(out_done, KD * (2 * j + 1))
                            for mt in range(KD):
                                last = products(ps_misc[:, mt, :], [(w_out_dt[:, mt * P:(mt + 1) * P], y_t[:, halves[q]])], first=mt == 0)
                            last.then_inc(out_sums, 1)

            run_turns(pe, turn)

        @block.scalar
        def _(act):
            nc.scalar.preload_act_table_set("natural_log_exp_and_others")
            act.wait_ge(small_loaded, 16)
            lg = logs[0:N_STATE, :]
            nc.scalar.activation(state_abs[:], lg, ACT.Abs).then_inc(prep_act, 1)
            act.wait_ge(prep_act, 1)
            nc.scalar.activation(state_exp[:], state_abs[:], ACT.Exp, scale=-1.0).then_inc(prep_act, 1)
            act.wait_ge(prep_act, 2)
            nc.scalar.activation(state_ln[:], state_exp[:], ACT.Ln, bias=1.0).then_inc(prep_act, 1)
            nc.scalar.preload_act_table_set("gelu_and_others")

            def weight_stage(j):
                act.wait_ge(stage_loaded[j % 2], 16 * (j // 2 + 1))
                nc.scalar.activation(w_hi[:, j * STAGE:(j + 1) * STAGE], stage[:, j % 2, :], ACT.Copy, scale=W_SCALE).then_inc(stage_hi, 1)

            def turn(t):
                for hf in range(2):
                    for m in range(UNITS):
                        s = m - CHAIN_AT
                        if t.at(0) and (UNITS * hf + m) % 3 == 1 and (UNITS * hf + m) // 3 < STAGES:
                            weight_stage((UNITS * hf + m) // 3)
                        if m == 0 and t.has(hf):
                            act.wait_ge(x_loaded[hf], 16 * (t.i + 1))
                            nc.scalar.activation(x_split[hf][0][:], x_in[hf][:], ACT.Copy).then_inc(x_hi_done, 1)
                        if 0 <= s < STEPS and t.has(hf):
                            c = t.chunk(hf)
                            act.wait_ge(rnn_sums, STEPS * c + s + 1)
                            to, at = (hf, cols[s + 1]) if s < STEPS - 1 else (1 - hf, cols[0])
                            nc.scalar.activation(h_split[to][0][:, :, at], ps_rnn[:, :, cols[s]], ACT.Tanh, scale=1.0 / W_SCALE).then_inc(h_hi_done, 1)
                            if s == STEPS - 1:
                                wait(act, x1_done, c)
                            nc.scalar.activation(h_rnn[to][:, :, at], ps_rnn[:, :, cols[s]], ACT.Tanh, scale=1.0 / W_SCALE).then_inc(h_ready, 1)
                        if m == X2_AT + 1 and t.has(hf - 1):
                            c = t.chunk(hf - 1)
                            act.wait_ge(x2_done, c + 1)
                            wait(act, hidden, UNITS * (c - 1))
                            nc.scalar.activation(x2_split[1 - hf][0][:], x2[1 - hf][:], ACT.Copy).then_inc(x2_hi_done, 1)
                        if m >= 1 and t.has(hf - 2) or m == 0 and t.has(hf - 3):
                            c = t.chunk(hf - 2) if m else t.chunk(hf - 3)
                            n = (m - 1) % UNITS
                            if n < SHARED_UNITS:
                                act.wait_ge(evacuated, SHARED_UNITS * c + n + 1)
                            else:
                                act.wait_ge(gated, N_ROUTED * c + n - SHARED_UNITS + 1)
                            wait(act, summed, UNITS * c + n - SPLITS + 1)
                            nc.scalar.activation(hid_hi[n % SPLITS][:], hid[n % HIDS][:], ACT.Copy).then_inc(hi_done, 1)
                        if hf == 0 and m in (5, 6) and t.has_pair(-3):
                            j, q = t.i - 3, m - 5
                            act.wait_ge(post_sums, 2 * j + q + 1)
                            if q == 0:
                                wait(act, post_ops, POST_OPS * j)
                            nc.scalar.activation(z_b[:, halves[q]], ps_misc[0:N_STATE, 0, :], ACT.Identity, bias=proj_bias[0:N_STATE, :]).then_inc(post_copied, 1)
                            nc.scalar.activation(c_t[:, halves[q]], ps_misc[N_STATE:P, 0, :], ACT.Tanh, bias=proj_bias[N_STATE:P, :]).then_inc(post_copied, 1)
                            nc.scalar.activation(u_t[:, halves[q]], ps_misc[0:N_STATE, 1, :], ACT.Identity, bias=skip_bias[0:N_STATE, :]).then_inc(post_copied, 1)
                        if hf == 1 and m == 0 and t.has_pair(-3):
                            j = t.i - 3
                            act.wait_ge(post_copied, 3 * (2 * j + 2))
                            nc.scalar.activation(z_abs[:], z_b[:], ACT.Abs).then_inc(post_act, 1)
                            nc.scalar.preload_act_table_set("natural_log_exp_and_others")
                            act.wait_ge(post_act, 3 * j + 1)
                            nc.scalar.activation(z_exp[:], z_abs[:], ACT.Exp, scale=-1.0).then_inc(post_act, 1)
                            act.wait_ge(post_act, 3 * j + 2)
                            nc.scalar.activation(z_ln[:], z_exp[:], ACT.Ln, bias=1.0).then_inc(post_act, 1)
                            if not t.has(hf - 2):
                                nc.scalar.preload_act_table_set("gelu_and_others")
                        if m == 0 and t.has(hf - 2):
                            nc.scalar.preload_act_table_set("silu_and_others")
                        if m == SHARED_UNITS and t.has(hf - 2):
                            nc.scalar.preload_act_table_set("gelu_and_others")
                        if hf == 0 and m in SHIFT_AT and t.has_pair(-2):
                            j, part_ = t.i - 2, SHIFT_AT.index(m)
                            mid = HIST // 2
                            if part_ == 0:
                                wait(act, taps_done, TAP_OPS * j)
                                nc.scalar.activation(hist[:, :, 0:mid], hist[:, :, PAIR:PAIR + mid], ACT.Copy).then_inc(hist_moved, 1)
                            if part_ == 1:
                                act.wait_ge(hist_moved, 2 * j + 1)
                                wait(act, out_done, KD * 2 * (j - 1))
                                nc.scalar.activation(hist[:, :, mid:HIST], hist[:, :, PAIR + mid:PAIR + HIST], ACT.Copy).then_inc(hist_moved, 1)
                            if part_ == 2:
                                act.wait_ge(x3_done, 2 * (j + 1))
                                act.wait_ge(hist_moved, 2 * j + 2)
                                wait(act, post_sums, 2 * j)
                                nc.scalar.activation(hist[:, :, HIST:], x3_new[:], ACT.Copy).then_inc(hist_ready, 1)
                        if t.has(hf - 2):
                            c = t.chunk(hf - 2)
                            if m == 1:
                                act.wait_ge(gate_ops, GATE_OPS * c + 1)
                                nc.scalar.activation(half_scores[:], logits[:], ACT.Tanh, scale=0.5).then_inc(scored, 1)
                            act.wait_ge(hidden, UNITS * c + m + 1)
                            if m < SHARED_UNITS:
                                wait(act, evacuated, SHARED_UNITS * c + m - 1)
                                nc.scalar.activation(act_f[m % 2][:], ps_hid[(2 * m) % BANKS][:], ACT.Silu, scale=1.0 / W_SCALE).then_inc(activated, 1)
                            else:
                                act.wait_ge(lo_done, UNITS * c + m - HIDS + 1)
                                nc.scalar.activation(hid[m % HIDS][:], ps_hid[(SHARED_UNITS + m) % BANKS][:], ACT.Gelu, scale=1.0 / W_SCALE).then_inc(activated, 1)
                        if m == X1_AT + 1 and t.has(hf):
                            c = t.chunk(hf)
                            act.wait_ge(x1_done, c + 1)
                            wait(act, spike_sums, STEPS * (c - 2) + 1)
                            nc.scalar.activation(x1_split[hf][0][:], x1[hf][:], ACT.Copy).then_inc(x1_hi_done, 1)

            run_turns(act, turn)

        @block.vector
        def _(dve):
            n_prep = [0]

            def prepared(ins):
                n_prep[0] += 1
                ins.then_inc(prep, 1)
                dve.wait_ge(prep, n_prep[0])

            n_rnn = [0]

            def split(halves_, source, scale, count):
                count(nc.vector.tensor_scalar(halves_[0][:], source, scale, None, ALU.mult))
                count(nc.vector.scalar_tensor_tensor(halves_[1][:], source, scale, halves_[0][:], ALU.mult, ALU.subtract))

            def rnn_prepared(ins):
                n_rnn[0] += 1
                ins.then_inc(rnn_prep, 1)
                dve.wait_ge(rnn_prep, n_rnn[0])

            dve.wait_ge(first_loaded, 16)
            nc.vector.tensor_copy(h_rnn[0][:, :, cols[0]], cond).then_inc(h_start, 1)
            split(cond_split, cond, 1.0, rnn_prepared)
            split(wx_split, wx, W_SCALE, rnn_prepared)
            split(wh_split, wh, W_SCALE, rnn_prepared)
            nc.vector.tensor_scalar(u_mem[:], cond, W_SCALE, None, ALU.mult).then_inc(rnn_weights, 1)
            dve.wait_ge(small_loaded, 16)
            prepared(nc.vector.tensor_scalar(a_col[:], alpha_col[:, :, 0], A_LO, A_HI, ALU.max, ALU.min))
            prepared(nc.vector.tensor_scalar(a_row[:], alpha_row, A_LO, A_HI, ALU.max, ALU.min))
            prepared(nc.vector.tensor_scalar(keep_row[:], a_row[:], -W_SCALE, W_SCALE, ALU.mult, ALU.add))
            prepared(nc.vector.tensor_scalar(a_row[:], a_row[:], W_SCALE, None, ALU.mult))
            both = lambda row: row[:].rearrange("p (k n) -> p k n", k=1).broadcast_to((P, KD, D))
            prepared(nc.vector.tensor_tensor(w_spike[:], w_in, both(keep_row), ALU.mult))
            prepared(nc.vector.tensor_tensor(v_in, v_in, off_diag, ALU.mult))
            prepared(nc.vector.tensor_tensor(v_in, v_in, both(keep_row), ALU.mult))
            prepared(nc.vector.tensor_scalar(on_diag[:], off_diag, -1.0, None, ALU.add))
            prepared(nc.vector.tensor_tensor(on_diag[:], on_diag[:], both(a_row), ALU.mult))
            prepared(nc.vector.tensor_tensor(v_in, v_in, on_diag[:], ALU.add))
            split(w_spike_split, w_spike[:], 1.0, prepared)
            split(v_split, v_in, 1.0, prepared)
            split(router_split, router[:, 0:KD, :], W_SCALE, prepared)
            dve.wait_ge(cond_mm, 1)
            prepared(nc.vector.tensor_copy(cond_logits[:], ps_misc[:, 0, 0:N_ROUTED]))
            dve.wait_ge(prep_act, 3)
            prepared(nc.vector.scalar_tensor_tensor(state_sp[:], logs[0:N_STATE, :], 0.0, state_ln[:], ALU.max, ALU.add))
            prepared(nc.vector.tensor_tensor(step_a[:], state_sp[:, 0:1], state_sp[:, 1:2], ALU.mult))
            assert n_prep[0] == PREP_OPS
            prepared(nc.vector.tensor_scalar(decay[:], step_a[:], -1.0, 1.0, ALU.mult, ALU.add))
            prepared(nc.vector.memset(decay_run[:], 1.0))
            prepared(nc.vector.tensor_scalar(decay_run[:], decay_run[:], decay[:, 0:1], None, ALU.mult))
            prepared(nc.vector.memset(decay_run[:, :, 0:1], 0.0))
            prepared(nc.vector.tensor_scalar(w_out_dt[:], w_out[0:N_STATE, :], state_sp[:, 1:2], None, ALU.mult))
            prepared(nc.vector.memset(state[:], 0.0))

            def weight_stage(j):
                dve.wait_ge(stage_hi, j + 1)
                nc.vector.scalar_tensor_tensor(w_lo[:, j * STAGE:(j + 1) * STAGE], stage[:, j % 2, :], W_SCALE,
                                               w_hi[:, j * STAGE:(j + 1) * STAGE], ALU.mult, ALU.subtract).then_inc(stage_lo, 1)

            def spike_step(c, s, par):
                dve.wait_ge(spike_sums, STEPS * c + s + 1)
                for kd in range(KD):
                    nc.vector.scalar_tensor_tensor(u_mem[:, kd, :], u_mem[:, kd, :], a_col[:, kd:kd + 1], ps_spike[:, kd, cols[s]], ALU.mult, ALU.add).then_inc(membrane, 1)
                if s == 0:
                    wait(dve, x2_done, c - 1)
                dve.wait_ge(membrane, KD * (STEPS * c + s + 1))
                nc.vector.tensor_scalar(spikes[par][:, :, cols[s]], u_mem[:], W_SCALE, None, ALU.is_gt).then_inc(spiked, 1)

            def unit_evacuate(c, m):
                wait(dve, lo_done, UNITS * c + m - HIDS + 1)
                dve.wait_ge(activated, UNITS * c + m + 1)
                nc.vector.scalar_tensor_tensor(hid[m % HIDS][:], ps_hid[(2 * m + 1) % BANKS][:], H_SCALE / (N_SHARED * LAYER * W_SCALE),
                                               act_f[m % 2][:], ALU.mult, ALU.mult).then_inc(evacuated, 1)

            def choose_experts(c, between):
                done = [1]

                def step(ins):
                    done[0] += 1
                    ins.then_inc(gate_ops, 1)

                def settle():
                    between()
                    dve.wait_ge(gate_ops, GATE_OPS * c + done[0])

                def hold():
                    nc.vector.memset(dve_hold[:], 0.0)

                dve.wait_ge(scored, c + 1)
                step(nc.vector.tensor_scalar(scores[:], half_scores[:], 0.5, 0.5, ALU.mult, ALU.add))
                settle()
                step(nc.vector.tensor_tensor(select[:], scores[:], router_bias, ALU.add))
                settle()
                hold()
                for q in range(QB):
                    step(nc.vector.max(top[:, q, :], select[:, q, :]))
                settle()
                hold()
                for q in range(QB):
                    step(nc.vector.max_index(top_at[:, q, :], top[:, q, :], select[:, q, :]))
                settle()
                step(nc.vector.tensor_copy(top_at_f[:], top_at[:, :, 0:2]))
                settle()
                for q in range(QB):
                    step(nc.vector.tensor_scalar(chosen0[:, q, :], iota, top_at_f[:, q, 0:1], None, ALU.is_equal))
                settle()
                for q in range(QB):
                    step(nc.vector.scalar_tensor_tensor(chosen[:, q, :], iota, top_at_f[:, q, 1:2], chosen0[:, q, :], ALU.is_equal, ALU.add))
                assert done[0] == CHOICE_OPS, done[0]

            def make_gates(c, par, between):
                done = [CHOICE_OPS]

                def step(ins):
                    done[0] += 1
                    ins.then_inc(gate_ops, 1)

                def settle():
                    between()
                    dve.wait_ge(gate_ops, GATE_OPS * c + done[0])

                dve.wait_ge(gate_ops, GATE_OPS * c + CHOICE_OPS)
                step(nc.vector.tensor_tensor(picked[:], chosen[:], scores[:], ALU.mult))
                settle()
                step(nc.vector.tensor_reduce(denom[:], picked[:], AX_X, ALU.add))
                settle()
                step(nc.vector.tensor_scalar(denom_eps[:], denom[:], 1e-9, None, ALU.add))
                step(nc.vector.tensor_scalar(denom_ok[:], denom[:], 1e-9, None, ALU.is_gt))
                settle()
                unit = H_SCALE / LAYER
                step(nc.vector.reciprocal(denom_inv[:], denom_eps[:]))
                step(nc.vector.tensor_scalar(gate_even[:], denom_ok[:], -0.5 * unit, 0.5 * unit, ALU.mult, ALU.add))
                settle()
                step(nc.vector.scalar_tensor_tensor(gate_scale[:], denom_inv[:], unit, denom_ok[:], ALU.mult, ALU.mult))
                settle()
                for q in range(QB):
                    step(nc.vector.tensor_scalar(gate_a[:, q, :], scores[:, q, :], gate_scale[:, q:q + 1], gate_even[:, q:q + 1], ALU.mult, ALU.add))
                settle()
                wait(dve, gates_stored, 16 * (c - 1))
                step(nc.vector.tensor_tensor(gates[par][:], gate_a[:], chosen[:], ALU.mult))
                assert done[0] == GATE_OPS, done[0]

            def tap(j, n):
                k, kd = n // KD, n % KD
                window = hist[:, kd, k * B:k * B + PAIR]
                if k == 0:
                    if kd == 0:
                        dve.wait_ge(hist_ready, j + 1)
                        wait(dve, post_sums, 2 * j)
                    ins = nc.vector.tensor_scalar(conv[:, kd, :], window, cond[:, kd, 0:1], conv_bias[:, kd:kd + 1], ALU.mult, ALU.add)
                else:
                    dve.wait_ge(taps_done, TAP_OPS * j + n - KD + 1)
                    ins = nc.vector.scalar_tensor_tensor(conv[:, kd, :], window, cond[:, kd, k:k + 1], conv[:, kd, :], ALU.mult, ALU.add)
                ins.then_inc(taps_done, 1)

            def scan(j, between):
                by_time = lambda ap: ap.rearrange("p (t b) -> p t b", b=B)
                turned = lambda ap: ap[:].rearrange("p b t -> p t b")
                dve.wait_ge(post_act, 3 * (j + 1))
                nc.vector.scalar_tensor_tensor(b_t[:], z_b[:], 0.0, z_ln[:], ALU.max, ALU.add).then_inc(post_ops, 1)
                between()
                dve.wait_ge(post_ops, POST_OPS * j + 1)
                nc.vector.tensor_tensor(turned(drive), by_time(b_t[:]), by_time(u_t[:]), ALU.mult).then_inc(post_ops, 1)
                between()
                dve.wait_ge(post_ops, POST_OPS * j + 2)
                nc.vector.scalar_tensor_tensor(drive[:, :, 0], state[:, :, 2 * STEPS - 1], decay[:, 0:1], drive[:, :, 0], ALU.mult, ALU.add).then_inc(post_ops, 1)
                between()
                dve.wait_ge(post_ops, POST_OPS * j + 3)
                nc.vector.tensor_tensor_scan(state[:].rearrange("p b t -> p (b t)"), decay_run[:].rearrange("p b t -> p (b t)"),
                                             drive[:].rearrange("p b t -> p (b t)"), 0.0, ALU.mult, ALU.add).then_inc(post_ops, 1)
                between()
                dve.wait_ge(post_ops, POST_OPS * j + 4)
                wait(dve, out_sums, 2 * j)
                nc.vector.tensor_tensor(by_time(y_t[:]), by_time(c_t[:]), turned(state), ALU.mult).then_inc(post_ops, 1)

            def turn(t):
                for hf in range(2):
                    for m in range(UNITS):
                        s = m - CHAIN_AT
                        if t.at(0) and (UNITS * hf + m) % 3 == 1 and (UNITS * hf + m) // 3 < STAGES:
                            weight_stage((UNITS * hf + m) // 3)
                        if m == 1 and t.has(hf - 2):
                            c = t.chunk(hf - 2)
                            dve.wait_ge(router_sums, c + 1)
                            wait(dve, scored, c)
                            nc.vector.scalar_tensor_tensor(logits[:], ps_misc[:, 0, 0:QB * N_ROUTED].rearrange("p (q e) -> p q e", q=QB), 1.0 / W_SCALE,
                                                           cond_logits[:].rearrange("p (q e) -> p q e", q=1).broadcast_to((P, QB, N_ROUTED)), ALU.mult, ALU.add).then_inc(gate_ops, 1)
                        if m == LAG and t.has(hf - 3):
                            c = t.chunk(hf - 3)
                            dve.wait_ge(summed, UNITS * (c + 1))
                            wait(dve, hist_ready, t.i - 2 + hf)
                            nc.vector.scalar_tensor_tensor(x3_new[:, :, halves[1 - hf]], ps_y[:], Y_SCALE, x2[1 - hf][:], ALU.mult, ALU.add).then_inc(x3_done, 1)
                        if 0 <= s < STEPS and t.has(hf - 1):
                            spike_step(t.chunk(hf - 1), s, 1 - hf)
                        todo = [(t.i - 2, n) for n in taps_at(UNITS * hf + m)] if t.has_pair(-2) else []
                        if t.has_pair(-3):
                            todo = [(t.i - 3, n) for n in taps_at(UNITS * hf + m + 2 * UNITS)] + todo

                        def next_tap():
                            if todo:
                                tap(*todo.pop(0))

                        if m == 2 and t.has(hf - 2):
                            make_gates(t.chunk(hf - 2), hf, next_tap)
                        next_tap()
                        if m >= 1 and t.has(hf - 2) or m == 0 and t.has(hf - 3):
                            c = t.chunk(hf - 2) if m else t.chunk(hf - 3)
                            n = (m - 1) % UNITS
                            dve.wait_ge(hi_done, UNITS * c + n + 1)
                            nc.vector.tensor_tensor(hid_lo[n % SPLITS][:], hid[n % HIDS][:], hid_hi[n % SPLITS][:], ALU.subtract).then_inc(lo_done, 1)
                        if m == 1 and t.has(hf - 2):
                            choose_experts(t.chunk(hf - 2), next_tap)
                        if hf == 1 and m == SCAN_AT and t.has_pair(-3):
                            scan(t.i - 3, next_tap)
                        while todo:
                            next_tap()
                        if m < SHARED_UNITS and t.has(hf - 2):
                            unit_evacuate(t.chunk(hf - 2), m)
                        if hf == 1 and m in (5, 7) and t.has_pair(-3):
                            j, q = t.i - 3, (m - 5) // 2
                            dve.wait_ge(out_sums, 2 * j + q + 1)
                            wait(dve, out_stored, 16 * (2 * j))
                            at = HIST
                            if t.has_pair(-2):
                                dve.wait_ge(hist_ready, j + 2)
                                at = HIST - PAIR
                            for kd in range(KD):
                                nc.vector.scalar_tensor_tensor(out_sb[q][:, kd, :], ps_misc[:, kd, :], out_bias[:, kd:kd + 1],
                                                               hist[:, kd, at + q * TOK:at + (q + 1) * TOK], ALU.add, ALU.add).then_inc(out_done, 1)

            dve.wait_ge(pool_start, 1)
            run_turns(dve, turn)

        @block.gpsimd
        def _(pool):
            nc.gpsimd.memset(hist[:], 0.0).then_inc(pool_start, 1)
            pool.wait_ge(pool_start, 1)

            pool.wait_ge(h_start, 1)

            def turn(t):
                for hf in range(2):
                    for m in range(UNITS):
                        s = m - CHAIN_AT
                        if m == 0 and t.has(hf):
                            pool.wait_ge(x_hi_done, t.chunk(hf) + 1)
                            nc.gpsimd.tensor_tensor(x_split[hf][1][:], x_in[hf][:], x_split[hf][0][:], ALU.subtract).then_inc(x_lo_done, 1)
                        if 0 <= s < STEPS and t.has(hf):
                            to, at = (hf, cols[s + 1]) if s < STEPS - 1 else (1 - hf, cols[0])
                            pool.wait_ge(h_ready, STEPS * t.chunk(hf) + s + 1)
                            nc.gpsimd.tensor_tensor(h_split[to][1][:, :, at], h_rnn[to][:, :, at], h_split[to][0][:, :, at], ALU.subtract).then_inc(h_lo_done, 1)
                        if m == X2_AT and t.has(hf - 1):
                            c = t.chunk(hf - 1)
                            pool.wait_ge(spiked, STEPS * (c + 1))
                            wait(pool, x3_done, c - 1)
                            nc.gpsimd.tensor_tensor(x2[1 - hf][:], x1[1 - hf][:], spikes[1 - hf][:], ALU.add).then_inc(x2_done, 1)
                        if m == X2_AT + 1 and t.has(hf - 1):
                            c = t.chunk(hf - 1)
                            pool.wait_ge(x2_hi_done, c + 1)
                            nc.gpsimd.tensor_tensor(x2_split[1 - hf][1][:], x2[1 - hf][:], x2_split[1 - hf][0][:], ALU.subtract).then_inc(x2_lo_done, 1)
                        if m >= SHARED_UNITS and t.has(hf - 2):
                            c = t.chunk(hf - 2)
                            e = m - SHARED_UNITS
                            if e == 0:
                                pool.wait_ge(gates_loaded[hf], 16 * t.i)
                            pool.wait_ge(activated, UNITS * c + m + 1)
                            gate = gates_all[hf][:, :, e:e + 1].rearrange("p n o -> p o n").broadcast_to((P, 2, TOK))
                            nc.gpsimd.tensor_tensor(hid[m % HIDS][:], hid[m % HIDS][:], gate, ALU.mult).then_inc(gated, 1)
                        if m == X1_AT and t.has(hf):
                            c = t.chunk(hf)
                            pool.wait_ge(h_ready, STEPS * c + STEPS - 1)
                            pool.wait_ge(x_loaded[hf], 16 * (t.i + 1))
                            wait(pool, x2_done, c - 1)
                            nc.gpsimd.tensor_tensor(x1[hf][:], x_in[hf][:], h_rnn[hf][:], ALU.add).then_inc(x1_done, 1)
                        if m == 11 and t.has(hf):
                            pool.wait_ge(x1_hi_done, t.chunk(hf) + 1)
                            nc.gpsimd.tensor_tensor(x1_split[hf][1][:], x1[hf][:], x1_split[hf][0][:], ALU.subtract).then_inc(x1_lo_done, 1)

            run_turns(pool, turn)


def kernel(**inputs):
    import numpy as np
    import concourse.bacc as bacc
    from concourse.bass_utils import run_bass_kernel_spmd

    a = {k: np.asarray(v) for k, v in inputs.items()}

    def rows(w):
        n = w.shape[1]
        return w.reshape(-1, P, n).transpose(1, 0, 2).reshape(P, -1)

    def lay(v, width):
        full = np.zeros((P, width), np.float32)
        full[:v.shape[0], :v.shape[1]] = v
        return full

    c = a["cond_1024"]
    everywhere = lambda v: np.broadcast_to(v[None, :], (P, v.shape[0]))
    column = lambda v: v.reshape(-1, 1)
    alpha = a["L1_cond_alpha"]
    parts = {
        "wx": rows(a["L0_cond_Wx"].T), "wh": rows(a["L0_cond_Wh"].T), "cond": rows(c.T),
        "alpha_col": rows(np.broadcast_to(alpha[:, None], (D, B))),
        "w": rows(a["L1_cond_W"].T), "v": rows(a["L1_cond_V"]),
        "off_diag": rows(1.0 - np.eye(D, dtype=np.float32)), "alpha_row": everywhere(alpha),
        "cond4": rows(np.tile(c.T, (1, P // B))), "router": rows(a["L2_cond_W_router"].T),
        "router_bias": everywhere(np.tile(a["L2_cond_router_bias"], QB)),
        "iota": everywhere(np.arange(N_ROUTED, dtype=np.float32)),
        "proj": rows(a["L3_cond_Wp"]), "skip": rows(a["L3_cond_Ws"]), "out": lay(a["L3_cond_Wo"], D),
        "proj_bias": column(a["L3_cond_bp"]), "skip_bias": lay(column(a["L3_cond_bs"]), 1),
        "out_bias": rows(column(a["L3_cond_bo"])), "conv_bias": rows(column(a["L3_cond_conv_b"])),
        "logs": lay(np.stack([a["L3_cond_A_log"], a["L3_cond_dt_log"]], 1), 2),
    }
    small = np.ascontiguousarray(np.concatenate([parts[n] for n, _ in _SMALL], 1))
    experts = lambda w: np.concatenate([rows(w[e].T) for e in range(w.shape[0])], 1)
    big = np.ascontiguousarray(np.concatenate(
        [experts(a[f"L2_cond_{n}"]) for n in ("s_w1", "s_w3", "s_w2", "r_w1", "r_w2")], 1))
    x = np.ascontiguousarray(a["x"].transpose(2, 1, 0).reshape(KD, P, T * B).transpose(1, 0, 2))

    nc = bacc.Bacc("TRN2", target_bir_lowering=False, num_devices=1)
    arrays = {"x_t": x, "small_w": small, "big_w": big}
    args = [nc.dram_tensor(n, v.shape, F32, kind="ExternalInput").ap() for n, v in arrays.items()]
    args.append(nc.dram_tensor("out_t", (P, KD, T * B), F32, kind="ExternalOutput").ap())
    args.append(nc.dram_tensor("gates_scratch", (2, TOK, N_ROUTED), F32, kind="Internal").ap())
    build(nc, *args)
    r = run_bass_kernel_spmd(nc, [arrays], core_ids=[0])
    y = r.results[0]["out_t"]
    return np.ascontiguousarray(y.transpose(1, 0, 2).reshape(D, T, B).transpose(2, 1, 0))
```

```python
from contextlib import ExitStack

import concourse.bass as bass
from concourse import mybir

ALU = mybir.AluOpType
ACT = mybir.ActivationFunctionType
AX_X = mybir.AxisListType.X
F32 = mybir.dt.float32
F16 = mybir.dt.float16
U32 = mybir.dt.uint32

P = 128
B, T, D = 32, 256, 256
KD = D // P
N_SHARED, FF_SHARED = 2, 512
N_ROUTED, FF_ROUTED = 8, 256
N_STATE = 64
TAPS = B

STEPS = 8
TOK = STEPS * B
CHUNKS = T // STEPS
PAIRS = CHUNKS // 2
PAIR = 2 * TOK
HIST = (TAPS - 1) * B
QB = TOK // P

SHARED_UNITS = N_SHARED * FF_SHARED // (2 * P)
UNITS = SHARED_UNITS + N_ROUTED
BANKS = 3
LAG = 4
CHAIN_AT = 1

W_SCALE = 64.0
H_SCALE = 16.0
Y_SCALE = 1.0 / (W_SCALE * H_SCALE)
LAYER = 4.0

HIDS = 3
SPLITS = 6

GATE_OPS, CHOICE_OPS = 22, 12
HIST_TAPS = (HIST - PAIR) // B + 1
TAP_OPS = KD * TAPS
POST_OPS = 5

_SMALL = [
    ("wx", KD * D), ("wh", KD * D), ("cond", KD * B), ("alpha_col", KD * B),
    ("w", KD * D), ("v", KD * D), ("off_diag", KD * D), ("alpha_row", D),
    ("cond4", KD * P), ("router", 2 * KD * N_ROUTED), ("router_bias", QB * N_ROUTED),
    ("iota", N_ROUTED), ("proj", KD * 2 * N_STATE), ("skip", KD * N_STATE), ("out", D),
    ("proj_bias", 1), ("skip_bias", 1), ("out_bias", KD), ("conv_bias", KD),
    ("logs", 2),
]
SMALL = {}
_at = 0
for _n, _w in _SMALL:
    SMALL[_n] = (_at, _w)
    _at += _w
SMALL_COLS = _at
FIRST_COLS = SMALL["w"][0]

SW1, SW3, SW2 = 0, 2048, 4096
RW1 = 6144
RW2 = RW1 + N_ROUTED * KD * FF_ROUTED
BIG_COLS = RW2 + N_ROUTED * KD * FF_ROUTED
STAGE = 1024
STAGES = BIG_COLS // STAGE
STAGE_BUFS = 4
STAGE_SLOTS = [12, 13, 14, 22] + [2 * 12 + j for j in range(STAGES - 4)]

A_LO = 0.8187307530779818
A_HI = 0.9607894391523232


BANK_USES = 2 * SHARED_UNITS + N_ROUTED


def bank_at(par, use):
    return (use + par * BANK_USES) % BANKS


def use_of(m, part_=0):
    return 2 * m + part_ if m < SHARED_UNITS else SHARED_UNITS + m


def user_before(par, use):
    back, u, p = 0, use - 1, par
    while u >= 0 and bank_at(p, u) != bank_at(par, use):
        u -= 1
    if u < 0:
        back, u, p = 1, BANK_USES - 1, 1 - par
        while bank_at(p, u) != bank_at(par, use):
            u -= 1
    return (back, u // 2, u % 2 == 1) if u < 2 * SHARED_UNITS else (back, u - SHARED_UNITS, False)


X2_AT = 8
X1_AT = 9
CONV_AT = 4
POST_AT = (5, 6)
SHIFT_AT = (4, 5, 6)


def post_slots(t):
    return (8, 9, (12, 13)) if t.at(TURNS - 2) else (12, 17, (20, 22))


_TAPS = [0, 0, 0, 0, 0, 4, 5, 2, 2, 3, 3, 4,
         7, 2, 1, 2, 1, 1, 1, 2, 2, 3, 3, 4,
         7, 2, 1, 2]
_TAPS_LATE = [0, 0, 0, 0, 0, 3, 4, 2, 2, 3, 4, 4,
              7, 2, 1, 2, 2, 3, 3, 3, 4, 4, 4, 4,
              3]
_TAPS_LAST = [0, 0, 0, 0, 0, 6, 6, 6, 6, 5, 5, 4]
PE_FIRST_TAP, PE_TAP_OPS = 16, 26
DIAGONALS = 8
PE_TAPS_AT = 6
assert sum(_TAPS) == sum(_TAPS_LATE) == TAP_OPS and sum(_TAPS_LAST) == TAP_OPS - PE_TAP_OPS
assert PE_FIRST_TAP < KD * HIST_TAPS < PE_FIRST_TAP + PE_TAP_OPS and len(_TAPS) <= 2 * UNITS + CONV_AT


def taps_at(slot, pair):
    table = {PAIRS - 2: _TAPS_LATE, PAIRS - 1: _TAPS_LAST}.get(pair, _TAPS)
    done = sum(table[:slot])
    return range(done, done + (table[slot] if slot < len(table) else 0))


def pe_taps_at(m):
    n = -(-PE_TAP_OPS // (UNITS - PE_TAPS_AT))
    return range(n * (m - PE_TAPS_AT), min(PE_TAP_OPS, n * (m - PE_TAPS_AT + 1))) if m >= PE_TAPS_AT else ()


def diagonals_at(m):
    if m == 0:
        return range(DIAGONALS)
    taps = pe_taps_at(m)
    return range(min(PE_TAP_OPS, taps[0] + DIAGONALS), min(PE_TAP_OPS, taps[-1] + 1 + DIAGONALS)) if taps else ()


class Turn:

    def __init__(self, i):
        self.i = i

    def chunk(self, offset):
        return self.i * 2 + offset

    def has(self, offset):
        return not isinstance(self.i, int) or 0 <= 2 * self.i + offset < CHUNKS

    def at(self, i):
        return isinstance(self.i, int) and self.i == i

    def has_pair(self, offset):
        return not isinstance(self.i, int) or 0 <= self.i + offset < PAIRS


FIRST_TURN, LAST_TURN = 4, PAIRS - 1
TURNS = PAIRS + 3


def run_turns(engine, body, first=FIRST_TURN, last=LAST_TURN):
    for i in range(first):
        body(Turn(i))
    with engine.Fori(first, last + 1) as i:
        body(Turn(i))
    for i in range(last + 1, TURNS):
        body(Turn(i))


def slot_stage(t, hf, m):
    slot = (t.i * 2 + hf) * UNITS + m if isinstance(t.i, int) else -1
    return STAGE_SLOTS.index(slot) if slot in STAGE_SLOTS else -1


def wait(engine, sem, value):
    if not isinstance(value, int) or value > 0:
        engine.wait_ge(sem, value)


def build(nc: bass.Bass, x_t: bass.AP, small_w: bass.AP, big_w: bass.AP, out_t: bass.AP, gates_dram: bass.AP):
    with ExitStack() as ctx:
        def sb(name, shape, dt=F32):
            return ctx.enter_context(nc.sbuf_tensor(name, shape, dt))

        def psum(name, shape):
            return ctx.enter_context(nc.psum_tensor(name, shape, F32))

        def sem(name):
            return ctx.enter_context(nc.semaphore(name))

        small = sb("small", [P, SMALL_COLS])

        def part(name, **axes):
            at, w = SMALL[name]
            ap = small[:, at:at + w]
            if not axes:
                return ap
            names = " ".join(axes)
            first = next(iter(axes))
            return ap.rearrange(f"p ({names}) -> p {names}", **{first: axes[first]})

        wx, wh = part("wx", k=KD, n=D), part("wh", k=KD, n=D)
        cond = part("cond", k=KD, b=B)
        alpha_col = part("alpha_col", k=KD, b=B)
        w_in, v_in, off_diag = part("w", k=KD, n=D), part("v", k=KD, n=D), part("off_diag", k=KD, n=D)
        alpha_row = part("alpha_row")
        cond4 = part("cond4", k=KD, n=P)
        router = part("router", k=2 * KD, e=N_ROUTED)
        router_bias = part("router_bias", q=QB, e=N_ROUTED)
        iota = part("iota")
        proj, skip = part("proj", k=KD, n=2 * N_STATE), part("skip", k=KD, n=N_STATE)
        w_out = part("out")
        proj_bias, skip_bias = part("proj_bias"), part("skip_bias")
        out_bias, conv_bias = part("out_bias"), part("conv_bias")
        logs = part("logs")

        w_hi = sb("w_hi", [P, BIG_COLS], F16)
        w_lo = sb("w_lo", [P, BIG_COLS], F16)
        wx_split = [sb(f"wx_split{j}", [P, KD, D], F16) for j in range(2)]
        wh_split = [sb(f"wh_split{j}", [P, KD, D], F16) for j in range(2)]
        w_spike = sb("w_spike", [P, KD, D])
        w_spike_split = [sb(f"w_spike_split{j}", [P, KD, D], F16) for j in range(2)]
        router_split = [sb(f"router_split{j}", [P, KD, N_ROUTED], F16) for j in range(2)]
        v_split = [sb(f"v_split{j}", [P, KD, D], F16) for j in range(2)]
        keep_row = sb("keep_row", [P, D])
        a_row = sb("a_row", [P, D])
        on_diag = sb("on_diag", [P, KD, D])
        a_col = sb("a_col", [P, KD])
        cond_split = [sb(f"cond_split{j}", [P, KD, B], F16) for j in range(2)]
        cond_logits = sb("cond_logits", [P, N_ROUTED])
        state_abs = sb("state_abs", [N_STATE, 2])
        state_exp = sb("state_exp", [N_STATE, 2])
        state_ln = sb("state_ln", [N_STATE, 2])
        state_sp = sb("state_sp", [N_STATE, 2])
        step_a = sb("step_a", [N_STATE, 1])
        decay = sb("decay", [N_STATE, 1])
        decay_run = sb("decay_run", [N_STATE, B, 2 * STEPS])
        w_out_dt = sb("w_out_dt", [N_STATE, D])

        x_in = [sb(f"x_in{p}", [P, KD, TOK]) for p in range(2)]
        h_rnn = [sb(f"h_rnn{p}", [P, KD, TOK]) for p in range(2)]
        x_split = [[sb(f"x_split{p}{j}", [P, KD, TOK], F16) for j in range(2)] for p in range(2)]
        h_split = [[sb(f"h_split{p}{j}", [P, KD, TOK], F16) for j in range(2)] for p in range(2)]
        x1_split = [[sb(f"x1_split{p}{j}", [P, KD, TOK], F16) for j in range(2)] for p in range(2)]
        x1 = [sb(f"x1_{p}", [P, KD, TOK]) for p in range(2)]
        diagonal = lambda n: x_in[n % DIAGONALS // 4][:].rearrange("p k (h n) -> p (k h) n", h=2)[:, n % 4, :]
        eye = on_diag[:, 0, 0:P]
        u_mem = sb("u_mem", [P, KD, B])
        spikes = [sb(f"spikes{p}", [P, KD, TOK], F16) for p in range(2)]
        x2 = [sb(f"x2_{p}", [P, KD, TOK]) for p in range(2)]
        x2_split = [[sb(f"x2_split{p}{j}", [P, KD, TOK], F16) for j in range(2)] for p in range(2)]
        act_f = [sb(f"act_f{j}", [P, 2, TOK]) for j in range(2)]
        hid = [sb(f"hid{j}", [P, 2, TOK]) for j in range(HIDS)]
        hid_hi = [sb(f"hid_hi{j}", [P, 2, TOK], F16) for j in range(SPLITS)]
        hid_lo = [sb(f"hid_lo{j}", [P, 2, TOK], F16) for j in range(SPLITS)]
        gates = [sb(f"gates{p}", [P, QB, N_ROUTED]) for p in range(2)]
        gates_all = [sb(f"gates_all{p}", [P, TOK, N_ROUTED])[:] for p in range(2)]
        logits = sb("logits", [P, QB, N_ROUTED])
        half_scores = sb("half_scores", [P, QB, N_ROUTED])
        scores = sb("scores", [P, QB, N_ROUTED])
        select = sb("select", [P, QB, N_ROUTED])
        dve_hold = sb("dve_hold", [P, 1])
        top = sb("top", [P, QB, 8])
        top_at = sb("top_at", [P, QB, 8], U32)
        top_at_f = sb("top_at_f", [P, QB, 2])
        chosen0 = sb("chosen0", [P, QB, N_ROUTED])
        chosen = sb("chosen", [P, QB, N_ROUTED])
        picked = sb("picked", [P, QB, N_ROUTED])
        denom = sb("denom", [P, QB])
        denom_eps = sb("denom_eps", [P, QB])
        denom_inv = sb("denom_inv", [P, QB])
        denom_ok = sb("denom_ok", [P, QB])
        gate_scale = sb("gate_scale", [P, QB])
        gate_even = sb("gate_even", [P, QB])
        gate_a = sb("gate_a", [P, QB, N_ROUTED])
        x3_new = sb("x3_new", [P, KD, PAIR])
        hist = sb("hist", [P, KD, HIST + PAIR])
        conv = sb("conv", [P, KD, PAIR])
        convolved = sb("convolved", [P, KD, PAIR])
        flat = lambda ap: ap[:].rearrange("p k n -> p (k n)")
        stage = [hist[:, 0, 0:STAGE], hist[:, 1, 0:STAGE], flat(conv), flat(convolved)]
        z_b = sb("z_b", [N_STATE, PAIR])
        c_t = sb("c_t", [N_STATE, PAIR])
        u_t = sb("u_t", [N_STATE, PAIR])
        z_soft = sb("z_soft", [N_STATE, PAIR])
        b_t = sb("b_t", [N_STATE, PAIR])
        drive = sb("drive", [N_STATE, B, 2 * STEPS])
        state = sb("state", [N_STATE, B, 2 * STEPS])
        y_t = sb("y_t", [N_STATE, PAIR])
        out_sb = [sb(f"out_sb{q}", [P, KD, TOK]) for q in range(2)]

        ps_rnn = psum("ps_rnn", [P, KD, TOK])
        ps_spike = psum("ps_spike", [P, KD, TOK])
        ps_y = psum("ps_y", [P, KD, TOK])
        ps_misc = psum("ps_misc", [P, KD, TOK])
        ps_conv = psum("ps_conv", [P, 1, PAIR])
        ps_hid = [psum(f"ps_hid{j}", [P, 2, TOK]) for j in range(BANKS)]

        ps_post = lambda t, q: ps_y if q == 1 and t.at(TURNS - 1) else ps_misc
        conv_part = lambda kd, last: ps_conv[:, 0, :] if kd == 0 and not last else conv[:, kd, :]

        first_loaded, small_loaded = sem("first_loaded"), sem("small_loaded")
        stage_loaded = [sem(f"stage_loaded{j}") for j in range(STAGE_BUFS)]
        stage_hi, stage_lo = sem("stage_hi"), sem("stage_lo")
        rnn_prep, rnn_weights = sem("rnn_prep"), sem("rnn_weights")
        h_start, hist_zeroed = sem("h_start"), sem("hist_zeroed")
        prep, prep_act, cond_mm = sem("prep"), sem("prep_act"), sem("cond_mm")
        x_loaded = [sem(f"x_loaded{p}") for p in range(2)]
        x_hi_done, x_lo_done = sem("x_hi_done"), sem("x_lo_done")
        rnn_sums, h_ready, h_hi_done, h_lo_done = sem("rnn_sums"), sem("h_ready"), sem("h_hi_done"), sem("h_lo_done")
        x1_done, x1_hi_done, x1_lo_done = sem("x1_done"), sem("x1_hi_done"), sem("x1_lo_done")
        spike_sums, membrane, spiked = sem("spike_sums"), sem("membrane"), sem("spiked")
        x2_done, x2_hi_done, x2_lo_done = sem("x2_done"), sem("x2_hi_done"), sem("x2_lo_done")
        router_sums, gate_ops, scored = sem("router_sums"), sem("gate_ops"), sem("scored")
        gates_stored = sem("gates_stored")
        gates_loaded = [sem(f"gates_loaded{p}") for p in range(2)]
        hidden, activated = sem("hidden"), sem("activated")
        evacuated, gated = sem("evacuated"), sem("gated")
        hi_done, lo_done, summed = sem("hi_done"), sem("lo_done"), sem("summed")
        x3_done, hist_moved, hist_ready = sem("x3_done"), sem("hist_moved"), sem("hist_ready")
        taps_done, conv_copied = sem("taps_done"), sem("conv_copied")
        diagonals, tap_sums = sem("diagonals"), sem("tap_sums")
        post_sums, post_copied, post_act = sem("post_sums"), sem("post_copied"), sem("post_act")
        post_ops, out_sums, out_done = sem("post_ops"), sem("out_sums"), sem("out_done")
        out_stored = sem("out_stored")

        cols = [slice(s * B, (s + 1) * B) for s in range(STEPS)]
        halves = [slice(q * TOK, (q + 1) * TOK) for q in range(2)]
        PREP_OPS = 17
        block = ctx.enter_context(nc.Block())

        def sums_with_spikes(engine, t, hf, m):
            if m == X2_AT and t.has(hf - 1):
                c = t.chunk(hf - 1)
                engine.wait_ge(spiked, STEPS * (c + 1))
                engine.wait_ge(x1_done, c + 1)
                wait(engine, x3_done, c - 1)
                engine.tensor_tensor(x2[1 - hf][:], x1[1 - hf][:], spikes[1 - hf][:], ALU.add).then_inc(x2_done, 1)
            if m == X2_AT + 1 and t.has(hf - 1):
                engine.wait_ge(x2_hi_done, t.chunk(hf - 1) + 1)
                engine.tensor_tensor(x2_split[1 - hf][1][:], x2[1 - hf][:], x2_split[1 - hf][0][:], ALU.subtract).then_inc(x2_lo_done, 1)

        def sums_with_states(engine, t, hf, m):
            if m == X1_AT and t.has(hf):
                c = t.chunk(hf)
                engine.wait_ge(h_ready, STEPS * c + STEPS - 1)
                engine.wait_ge(x_loaded[hf], 16 * (t.i + 1))
                wait(engine, x2_done, c - 1)
                engine.tensor_tensor(x1[hf][:], x_in[hf][:], h_rnn[hf][:], ALU.add).then_inc(x1_done, 1)
            if m == X1_AT + 2 and t.has(hf):
                engine.wait_ge(x1_hi_done, t.chunk(hf) + 1)
                engine.tensor_tensor(x1_split[hf][1][:], x1[hf][:], x1_split[hf][0][:], ALU.subtract).then_inc(x1_lo_done, 1)

        @block.sync
        def _(sp):
            sp.dma_start(small[:, 0:FIRST_COLS], small_w[:, 0:FIRST_COLS]).then_inc(first_loaded, 16)
            for c in range(2):
                sp.dma_start(x_in[c][:], x_t[:, :, c * TOK:(c + 1) * TOK]).then_inc(x_loaded[c], 16)
            sp.dma_start(small[:, FIRST_COLS:], small_w[:, FIRST_COLS:]).then_inc(small_loaded, 16)
            for j in range(STAGE_BUFS):
                sp.dma_start(stage[j], big_w[:, j * STAGE:(j + 1) * STAGE]).then_inc(stage_loaded[j], 16)

            def turn(t):
                for hf in range(2):
                    if t.has(hf - 2):
                        c = t.chunk(hf - 2)
                        sp.wait_ge(gate_ops, GATE_OPS * (c + 1))
                        sp.dma_start(gates_dram[hf].rearrange("(q p) e -> p q e", p=P), gates[hf][:]).then_inc(gates_stored, 16)
                        sp.wait_ge(gates_stored, 16 * (c + 1))
                        wait(sp, gated, N_ROUTED * (c - 1))
                        sp.dma_start(gates_all[hf], gates_dram[hf].rearrange("(o n) e -> o n e", o=1).broadcast_to((P, TOK, N_ROUTED))).then_inc(gates_loaded[hf], 16)
                    if t.has(hf) and t.has(hf + 2):
                        c = t.chunk(hf)
                        sp.wait_ge(x1_done, c + 1)
                        sp.dma_start(x_in[hf][:], x_t[:, :, bass.ds((c + 2) * TOK, TOK)]).then_inc(x_loaded[hf], 16)
                    if hf == 1 and t.has_pair(-3):
                        for q in range(2):
                            n = t.chunk(q - 6)
                            sp.wait_ge(out_done, KD * (n + 1))
                            sp.dma_start(out_t[:, :, bass.ds(n * TOK, TOK)], out_sb[q][:]).then_inc(out_stored, 16)

            run_turns(sp, turn, last=LAST_TURN - 1)
            sp.wait_ge(out_stored, 16 * CHUNKS)

        @block.tensor
        def _(pe):
            PASSES = ((0, 0), (0, 1), (1, 0))

            def products(out, pairs, first=True):
                last = None
                for j, (w, v) in enumerate(pairs):
                    last = nc.tensor.matmul(out, w, v, start=first and j == 0, stop=j == len(pairs) - 1, skip_group_check=True)
                return last

            def project(ps, out_cols, weights, data, data_cols, first):
                passes = PASSES if len(data) == 2 else ((0, 0), (1, 0))
                for mt in range(KD):
                    last = products(ps[:, mt, out_cols], [
                        (weights[a][:, k, mt * P:(mt + 1) * P], data[b][:, k, data_cols])
                        for k in range(KD) for a, b in passes], first=first and mt == 0)
                return last

            def weights_split(cols_):
                pe.wait_ge(stage_lo, (cols_ + STAGE - 1) // STAGE)

            def unit_hidden(c, m, par):
                split = x2_split[par]
                w = (w_hi, w_lo)
                if m < SHARED_UNITS:
                    e, part_ = m // 2, m % 2
                    jobs = [(use_of(m, j), base + e * KD * FF_SHARED + part_ * 2 * P, FF_SHARED)
                            for j, base in enumerate((SW1, SW3))]
                else:
                    e = m - SHARED_UNITS
                    jobs = [(use_of(m), RW1 + e * KD * FF_ROUTED, FF_ROUTED)]
                for use, base, ff in jobs:
                    ps = ps_hid[bank_at(par, use)]
                    back, unit, evacuates = user_before(par, use)
                    if evacuates:
                        wait(pe, evacuated, SHARED_UNITS * (c - back) + unit + 1)
                    else:
                        wait(pe, activated, UNITS * (c - back) + unit + 1)
                    for ft in range(2):
                        last = products(ps[:, ft, :], [
                            (w[a][:, base + k * ff + ft * P:base + k * ff + (ft + 1) * P], split[b][:, k, :])
                            for k in range(KD) for a, b in PASSES], first=ft == 0)
                last.then_inc(hidden, 1)

            def unit_output(c, m):
                pe.wait_ge(lo_done, UNITS * c + m + 1)
                if m == 0:
                    wait(pe, x3_done, c)
                split = (hid_hi[m % SPLITS], hid_lo[m % SPLITS])
                w = (w_hi, w_lo)
                base = SW2 + m * 2 * D if m < SHARED_UNITS else RW2 + (m - SHARED_UNITS) * KD * D
                for mt in range(KD):
                    last = products(ps_y[:, mt, :], [
                        (w[a][:, base + f * D + mt * P:base + f * D + (mt + 1) * P], split[b][:, f, :])
                        for f in range(2) for a, b in PASSES], first=m == 0 and mt == 0)
                last.then_inc(summed, 1)

            pe.wait_ge(rnn_prep, 4)
            every = slice(0, TOK)

            def turn(t):
                out_at = post_slots(t)[2]
                for hf in range(2):
                    for m in range(UNITS):
                        s, slot = m - CHAIN_AT, UNITS * hf + m
                        if t.at(0) and hf == 0 and m == 1:
                            pe.wait_ge(small_loaded, 16)
                            products(ps_misc[:, 0, 0:N_ROUTED], [(cond4[:, k, :], router[:, KD + k, :]) for k in range(KD)]).then_inc(cond_mm, 1)
                        if 0 <= s < STEPS and t.has(hf):
                            c = t.chunk(hf)
                            data, at = (cond_split, slice(0, B)) if t.at(0) and hf == 0 and s == 0 else (h_split[hf], cols[s])
                            if t.at(0) and hf == 0 and s == 0:
                                pe.wait_ge(rnn_weights, 1)
                            wait(pe, h_lo_done, STEPS * c + s)
                            project(ps_rnn, cols[s], wh_split, data, at, first=False).then_inc(rnn_sums, 1)
                        if 0 <= s < STEPS and t.has(hf - 1):
                            c = t.chunk(hf - 1)
                            if t.at(0) and s == 0:
                                data, at = cond_split, slice(0, B)
                            else:
                                wait(pe, spiked, STEPS * c + s)
                                data, at = [spikes[1 - hf] if s else spikes[hf]], cols[s - 1]
                            project(ps_spike, cols[s], v_split, data, at, first=False).then_inc(spike_sums, 1)
                        if t.has(hf - 2):
                            c = t.chunk(hf - 2)
                            if m == 0:
                                pe.wait_ge(x2_lo_done, c + 1)
                            if t.at(1) and hf == 0:
                                weights_split(SW3 + (m // 2 + 1) * KD * FF_SHARED if m < SHARED_UNITS else RW1 + (m - SHARED_UNITS + 1) * KD * FF_ROUTED)
                            unit_hidden(c, m, hf)
                        if t.at(1) and 0 <= UNITS * hf + m - LAG < UNITS:
                            n = UNITS * hf + m - LAG
                            weights_split(SW2 + (n + 1) * 2 * D if n < SHARED_UNITS else RW2 + (n - SHARED_UNITS + 1) * KD * D)
                        if m >= LAG and t.has(hf - 2):
                            unit_output(t.chunk(hf - 2), m - LAG)
                        if m < LAG and t.has(hf - 3):
                            unit_output(t.chunk(hf - 3), UNITS + m - LAG)
                        if m == 0 and t.has(hf - 2):
                            c = t.chunk(hf - 2)
                            wait(pe, gate_ops, GATE_OPS * (c - 1) + 1)
                            if hf == 1 and t.has_pair(-3):
                                pe.wait_ge(post_copied, 3 * t.chunk(-4))
                            if hf == 0 and t.has_pair(-4):
                                pe.wait_ge(out_done, KD * t.chunk(-6))
                            for q in range(QB):
                                last = products(ps_misc[:, 0, q * N_ROUTED:(q + 1) * N_ROUTED],
                                                [(x2_split[hf][a][:, k, q * P:(q + 1) * P], router_split[b][:, k, :])
                                                 for k in range(KD) for a, b in PASSES], first=q == 0)
                            last.then_inc(router_sums, 1)
                        if m == 0 and t.has(hf - 1):
                            c = t.chunk(hf - 1)
                            if t.at(0):
                                pe.wait_ge(prep, PREP_OPS)
                            pe.wait_ge(x1_lo_done, c + 1)
                            wait(pe, spiked, STEPS * c)
                            project(ps_spike, every, w_spike_split, x1_split[1 - hf], every, first=True)
                        if m == 0 and t.has(hf):
                            c = t.chunk(hf)
                            pe.wait_ge(x_lo_done, c + 1)
                            wait(pe, h_ready, STEPS * c)
                            project(ps_rnn, every, wx_split, x_split[hf], every, first=True)
                        if hf == 0 and m in POST_AT and t.has_pair(-3):
                            j, q = t.i - 3, POST_AT.index(m)
                            pe.wait_ge(conv_copied, KD * (j + 1))
                            if q == 0:
                                pe.wait_ge(gate_ops, GATE_OPS * t.chunk(-2) + 1 if t.has(-2) else GATE_OPS * CHUNKS)
                                wait(pe, out_done, KD * 2 * j)
                            elif t.at(TURNS - 1):
                                pe.wait_ge(x3_done, CHUNKS)
                            else:
                                pe.wait_ge(post_copied, 3 * (2 * j + 1))
                            ps = ps_post(t, q)
                            products(ps[:, 0, :], [(proj[:, k, :], convolved[:, k, halves[q]]) for k in range(KD)])
                            products(ps[0:N_STATE, 1, :], [(skip[:, k, :], hist[:, k, HIST + q * TOK:HIST + (q + 1) * TOK]) for k in range(KD)], first=False).then_inc(post_sums, 1)
                        if t.at(TURNS - 2) and hf == 0:
                            for n in pe_taps_at(m):
                                k, kd = (PE_FIRST_TAP + n) // KD, n % KD
                                if n == 0:
                                    pe.wait_ge(activated, UNITS * CHUNKS)
                                    pe.wait_ge(hist_moved, 2 * PAIRS)
                                if PE_FIRST_TAP + n == KD * HIST_TAPS:
                                    pe.wait_ge(hist_ready, PAIRS)
                                pe.wait_ge(diagonals, n + 1)
                                nc.tensor.matmul(flat(ps_hid[kd]), diagonal(n), hist[:, kd, k * B:k * B + PAIR],
                                                 start=n < KD, stop=n >= PE_TAP_OPS - KD, skip_group_check=True).then_inc(tap_sums, 1)
                        if slot in out_at and t.has_pair(-3):
                            j, q = t.i - 3, out_at.index(slot)
                            if q == 0:
                                pe.wait_ge(post_copied, 3 * (2 * j + 2))
                                if t.has(-1):
                                    pe.wait_ge(gate_ops, GATE_OPS * t.chunk(-1) + 1)
                                pe.wait_ge(post_ops, POST_OPS * (j + 1))
                            elif not t.at(TURNS - 1):
                                pe.wait_ge(out_done, KD * (2 * j + 1))
                            for mt in range(KD):
                                last = products(ps_post(t, q)[:, mt, :], [(w_out_dt[:, mt * P:(mt + 1) * P], y_t[:, halves[q]])], first=mt == 0)
                            last.then_inc(out_sums, 1)

            run_turns(pe, turn)

        @block.scalar
        def _(act):
            nc.scalar.preload_act_table_set("gelu_and_others")

            def state_logs():
                nc.scalar.preload_act_table_set("natural_log_exp_and_others")
                nc.scalar.activation(state_abs[:], logs[0:N_STATE, :], ACT.Abs).then_inc(prep_act, 1)
                act.wait_ge(prep_act, 1)
                nc.scalar.activation(state_exp[:], state_abs[:], ACT.Exp, scale=-1.0).then_inc(prep_act, 1)
                act.wait_ge(prep_act, 2)
                nc.scalar.activation(state_ln[:], state_exp[:], ACT.Ln, bias=1.0).then_inc(prep_act, 1)

            def stage_load(j):
                b = j % STAGE_BUFS
                act.wait_ge(stage_hi, j - STAGE_BUFS + 1)
                act.wait_ge(stage_lo, j - STAGE_BUFS + 1)
                nc.scalar.dma_start(stage[b], big_w[:, j * STAGE:(j + 1) * STAGE]).then_inc(stage_loaded[b], 16)

            def read_vector(t, q):
                nc.scalar.activation(c_t[:, halves[q]], ps_post(t, q)[N_STATE:P, 0, :], ACT.Tanh, bias=proj_bias[N_STATE:P, :]).then_inc(post_copied, 1)

            def weight_stage(j):
                act.wait_ge(stage_loaded[j % STAGE_BUFS], 16 * (j // STAGE_BUFS + 1))
                nc.scalar.activation(w_hi[:, j * STAGE:(j + 1) * STAGE], stage[j % STAGE_BUFS], ACT.Copy, scale=W_SCALE).then_inc(stage_hi, 1)

            def turn(t):
                soft_at = post_slots(t)[0]
                for hf in range(2):
                    for m in range(UNITS):
                        s, slot = m - CHAIN_AT, UNITS * hf + m
                        if t.at(1) and hf == 1 and m == 0:
                            state_logs()
                        if m == 0 and t.has(hf):
                            act.wait_ge(x_loaded[hf], 16 * (t.i + 1))
                            nc.scalar.activation(x_split[hf][0][:], x_in[hf][:], ACT.Copy).then_inc(x_hi_done, 1)
                        if 0 <= s < STEPS and t.has(hf):
                            c = t.chunk(hf)
                            act.wait_ge(rnn_sums, STEPS * c + s + 1)
                            to, at = (hf, cols[s + 1]) if s < STEPS - 1 else (1 - hf, cols[0])
                            nc.scalar.activation(h_split[to][0][:, :, at], ps_rnn[:, :, cols[s]], ACT.Tanh, scale=1.0 / W_SCALE).then_inc(h_hi_done, 1)
                            if s == STEPS - 1:
                                wait(act, x1_done, c)
                            nc.scalar.activation(h_rnn[to][:, :, at], ps_rnn[:, :, cols[s]], ACT.Tanh, scale=1.0 / W_SCALE).then_inc(h_ready, 1)
                        if m == X2_AT + 1 and t.has(hf - 1):
                            c = t.chunk(hf - 1)
                            act.wait_ge(x2_done, c + 1)
                            wait(act, hidden, UNITS * (c - 1))
                            nc.scalar.activation(x2_split[1 - hf][0][:], x2[1 - hf][:], ACT.Copy).then_inc(x2_hi_done, 1)
                        if m >= 1 and t.has(hf - 2) or m == 0 and t.has(hf - 3):
                            c = t.chunk(hf - 2) if m else t.chunk(hf - 3)
                            n = (m - 1) % UNITS
                            if n < SHARED_UNITS:
                                act.wait_ge(evacuated, SHARED_UNITS * c + n + 1)
                            else:
                                act.wait_ge(gated, N_ROUTED * c + n - SHARED_UNITS + 1)
                            wait(act, summed, UNITS * c + n - SPLITS + 1)
                            nc.scalar.activation(hid_hi[n % SPLITS][:], hid[n % HIDS][:], ACT.Copy).then_inc(hi_done, 1)
                        if hf == 0 and m - 1 in POST_AT and t.has_pair(-3):
                            j, q = t.i - 3, POST_AT.index(m - 1)
                            act.wait_ge(post_sums, 2 * j + q + 1)
                            if q == 0:
                                wait(act, post_ops, POST_OPS * j)
                            ps = ps_post(t, q)
                            nc.scalar.activation(z_b[:, halves[q]], ps[0:N_STATE, 0, :], ACT.Identity, bias=proj_bias[0:N_STATE, :]).then_inc(post_copied, 1)
                            nc.scalar.activation(u_t[:, halves[q]], ps[0:N_STATE, 1, :], ACT.Identity, bias=skip_bias[0:N_STATE, :]).then_inc(post_copied, 1)
                            if not t.at(TURNS - 1):
                                read_vector(t, q)
                        if t.at(TURNS - 1) and hf == 0 and m == 0:
                            nc.scalar.preload_act_table_set("natural_log_exp_and_others")
                        if slot == soft_at and t.has_pair(-3):
                            j = t.i - 3
                            act.wait_ge(post_copied, 3 * 2 * j + 4 if t.at(TURNS - 1) else 3 * (2 * j + 2))
                            nc.scalar.activation(z_soft[:], z_b[:], ACT.Abs).then_inc(post_act, 1)
                            nc.scalar.preload_act_table_set("natural_log_exp_and_others")
                            act.wait_ge(post_act, 3 * j + 1)
                            nc.scalar.activation(z_soft[:], z_soft[:], ACT.Exp, scale=-1.0).then_inc(post_act, 1)
                            act.wait_ge(post_act, 3 * j + 2)
                            nc.scalar.activation(z_soft[:], z_soft[:], ACT.Ln, bias=1.0).then_inc(post_act, 1)
                            if not t.has(hf - 2):
                                nc.scalar.preload_act_table_set("gelu_and_others")
                            if t.at(TURNS - 1):
                                for q in range(2):
                                    read_vector(t, q)
                        if m == 0 and t.has(hf - 2):
                            nc.scalar.preload_act_table_set("silu_and_others")
                        if t.at(TURNS - 2) and hf == 0:
                            for n in diagonals_at(m):
                                if n == 0:
                                    act.wait_ge(x1_done, CHUNKS)
                                wait(act, tap_sums, n - DIAGONALS + 1)
                                nc.scalar.activation(diagonal(n), eye, ACT.Identity, scale=cond[:, n % KD, (PE_FIRST_TAP + n) // KD:(PE_FIRST_TAP + n) // KD + 1]).then_inc(diagonals, 1)
                        if hf == 0 and m == CONV_AT and t.has_pair(-3) and not t.at(TURNS - 1):
                            j = t.i - 3
                            act.wait_ge(taps_done, TAP_OPS * (j + 1))
                            for kd in range(KD):
                                nc.scalar.activation(convolved[:, kd, :], conv_part(kd, False), ACT.Copy).then_inc(conv_copied, 1)
                        if m == SHARED_UNITS and t.has(hf - 2):
                            nc.scalar.preload_act_table_set("gelu_and_others")
                        if t.has(hf - 2):
                            c = t.chunk(hf - 2)
                            if m == 1:
                                act.wait_ge(gate_ops, GATE_OPS * c + 1)
                                nc.scalar.activation(half_scores[:], logits[:], ACT.Tanh, scale=0.5).then_inc(scored, 1)
                            act.wait_ge(hidden, UNITS * c + m + 1)
                            if m < SHARED_UNITS:
                                wait(act, evacuated, SHARED_UNITS * c + m - 1)
                                nc.scalar.activation(act_f[m % 2][:], ps_hid[bank_at(hf, use_of(m))][:], ACT.Silu, scale=1.0 / W_SCALE).then_inc(activated, 1)
                            else:
                                act.wait_ge(lo_done, UNITS * c + m - HIDS + 1)
                                nc.scalar.activation(hid[m % HIDS][:], ps_hid[bank_at(hf, use_of(m))][:], ACT.Gelu, scale=1.0 / W_SCALE).then_inc(activated, 1)
                        n = slot_stage(t, hf, m)
                        if n >= 1 and n + STAGE_BUFS - 1 < STAGES:
                            stage_load(n + STAGE_BUFS - 1)
                        if n >= 0:
                            weight_stage(n)
                        if hf == 0 and m in SHIFT_AT and t.has_pair(-2):
                            j, part_ = t.i - 2, SHIFT_AT.index(m)
                            mid = HIST // 2
                            if part_ == 0:
                                if t.at(2):
                                    act.wait_ge(hist_zeroed, 1)
                                wait(act, taps_done, TAP_OPS * j)
                                nc.scalar.activation(hist[:, :, 0:mid], hist[:, :, PAIR:PAIR + mid], ACT.Copy).then_inc(hist_moved, 1)
                            if part_ == 1:
                                act.wait_ge(hist_moved, 2 * j + 1)
                                wait(act, out_done, KD * 2 * (j - 1))
                                nc.scalar.activation(hist[:, :, mid:HIST], hist[:, :, PAIR + mid:PAIR + HIST], ACT.Copy).then_inc(hist_moved, 1)
                            if part_ == 2:
                                act.wait_ge(x3_done, 2 * (j + 1))
                                act.wait_ge(hist_moved, 2 * j + 2)
                                wait(act, post_sums, 2 * j)
                                nc.scalar.activation(hist[:, :, HIST:], x3_new[:], ACT.Copy).then_inc(hist_ready, 1)
                        if m == X1_AT + 1 and t.has(hf):
                            c = t.chunk(hf)
                            act.wait_ge(x1_done, c + 1)
                            wait(act, spike_sums, STEPS * (c - 2) + 1)
                            nc.scalar.activation(x1_split[hf][0][:], x1[hf][:], ACT.Copy).then_inc(x1_hi_done, 1)

            run_turns(act, turn)

        @block.vector
        def _(dve):
            n_prep = [0]

            def prepared(ins):
                n_prep[0] += 1
                ins.then_inc(prep, 1)
                dve.wait_ge(prep, n_prep[0])

            n_rnn = [0]

            def split(halves_, source, scale, count):
                count(nc.vector.tensor_scalar(halves_[0][:], source, scale, None, ALU.mult))
                count(nc.vector.scalar_tensor_tensor(halves_[1][:], source, scale, halves_[0][:], ALU.mult, ALU.subtract))

            def rnn_prepared(ins):
                n_rnn[0] += 1
                ins.then_inc(rnn_prep, 1)
                dve.wait_ge(rnn_prep, n_rnn[0])

            dve.wait_ge(first_loaded, 16)
            nc.vector.tensor_copy(h_rnn[0][:, :, cols[0]], cond).then_inc(h_start, 1)
            split(cond_split, cond, 1.0, rnn_prepared)
            split(wx_split, wx, W_SCALE, rnn_prepared)
            split(wh_split, wh, W_SCALE, rnn_prepared)
            nc.vector.tensor_scalar(u_mem[:], cond, W_SCALE, None, ALU.mult).then_inc(rnn_weights, 1)
            dve.wait_ge(small_loaded, 16)
            prepared(nc.vector.tensor_scalar(a_col[:], alpha_col[:, :, 0], A_LO, A_HI, ALU.max, ALU.min))
            prepared(nc.vector.tensor_scalar(a_row[:], alpha_row, A_LO, A_HI, ALU.max, ALU.min))
            prepared(nc.vector.tensor_scalar(keep_row[:], a_row[:], -W_SCALE, W_SCALE, ALU.mult, ALU.add))
            prepared(nc.vector.tensor_scalar(a_row[:], a_row[:], W_SCALE, None, ALU.mult))
            both = lambda row: row[:].rearrange("p (k n) -> p k n", k=1).broadcast_to((P, KD, D))
            prepared(nc.vector.tensor_tensor(w_spike[:], w_in, both(keep_row), ALU.mult))
            prepared(nc.vector.tensor_tensor(v_in, v_in, off_diag, ALU.mult))
            prepared(nc.vector.tensor_tensor(v_in, v_in, both(keep_row), ALU.mult))
            prepared(nc.vector.tensor_scalar(on_diag[:], off_diag, -1.0, None, ALU.add))
            prepared(nc.vector.tensor_tensor(on_diag[:], on_diag[:], both(a_row), ALU.mult))
            prepared(nc.vector.tensor_tensor(v_in, v_in, on_diag[:], ALU.add))
            split(w_spike_split, w_spike[:], 1.0, prepared)
            split(v_split, v_in, 1.0, prepared)
            split(router_split, router[:, 0:KD, :], W_SCALE, prepared)
            dve.wait_ge(cond_mm, 1)
            prepared(nc.vector.tensor_copy(cond_logits[:], ps_misc[:, 0, 0:N_ROUTED]))
            assert n_prep[0] == PREP_OPS

            def last_layer_constants():
                dve.wait_ge(prep_act, 3)
                prepared(nc.vector.scalar_tensor_tensor(state_sp[:], logs[0:N_STATE, :], 0.0, state_ln[:], ALU.max, ALU.add))
                prepared(nc.vector.tensor_tensor(step_a[:], state_sp[:, 0:1], state_sp[:, 1:2], ALU.mult))
                prepared(nc.vector.tensor_scalar(decay[:], step_a[:], -1.0, 1.0, ALU.mult, ALU.add))
                prepared(nc.vector.memset(decay_run[:], 1.0))
                prepared(nc.vector.tensor_scalar(decay_run[:], decay_run[:], decay[:, 0:1], None, ALU.mult))
                prepared(nc.vector.memset(decay_run[:, :, 0:1], 0.0))
                prepared(nc.vector.tensor_scalar(w_out_dt[:], w_out[0:N_STATE, :], state_sp[:, 1:2], None, ALU.mult))
                prepared(nc.vector.memset(state[:], 0.0))
                prepared(nc.vector.tensor_scalar(eye, off_diag[:, 0, 0:P], -1.0, 1.0, ALU.mult, ALU.add))

            def weight_stage(j):
                dve.wait_ge(stage_hi, j + 1)
                nc.vector.scalar_tensor_tensor(w_lo[:, j * STAGE:(j + 1) * STAGE], stage[j % STAGE_BUFS], W_SCALE,
                                               w_hi[:, j * STAGE:(j + 1) * STAGE], ALU.mult, ALU.subtract).then_inc(stage_lo, 1)

            def spike_step(c, s, par):
                dve.wait_ge(spike_sums, STEPS * c + s + 1)
                for kd in range(KD):
                    nc.vector.scalar_tensor_tensor(u_mem[:, kd, :], u_mem[:, kd, :], a_col[:, kd:kd + 1], ps_spike[:, kd, cols[s]], ALU.mult, ALU.add).then_inc(membrane, 1)
                if s == 0:
                    wait(dve, x2_done, c - 1)
                dve.wait_ge(membrane, KD * (STEPS * c + s + 1))
                nc.vector.tensor_scalar(spikes[par][:, :, cols[s]], u_mem[:], W_SCALE, None, ALU.is_gt).then_inc(spiked, 1)

            def unit_evacuate(c, m, par):
                wait(dve, lo_done, UNITS * c + m - HIDS + 1)
                dve.wait_ge(activated, UNITS * c + m + 1)
                nc.vector.scalar_tensor_tensor(hid[m % HIDS][:], ps_hid[bank_at(par, use_of(m, 1))][:], H_SCALE / (N_SHARED * LAYER * W_SCALE),
                                               act_f[m % 2][:], ALU.mult, ALU.mult).then_inc(evacuated, 1)

            def choose_experts(c, between):
                done = [1]

                def step(ins):
                    done[0] += 1
                    ins.then_inc(gate_ops, 1)

                def settle():
                    between()
                    dve.wait_ge(gate_ops, GATE_OPS * c + done[0])

                def hold():
                    nc.vector.memset(dve_hold[:], 0.0)

                dve.wait_ge(scored, c + 1)
                step(nc.vector.tensor_scalar(scores[:], half_scores[:], 0.5, 0.5, ALU.mult, ALU.add))
                settle()
                step(nc.vector.tensor_tensor(select[:], scores[:], router_bias, ALU.add))
                settle()
                hold()
                for q in range(QB):
                    step(nc.vector.max(top[:, q, :], select[:, q, :]))
                settle()
                hold()
                for q in range(QB):
                    step(nc.vector.max_index(top_at[:, q, :], top[:, q, :], select[:, q, :]))
                settle()
                step(nc.vector.tensor_copy(top_at_f[:], top_at[:, :, 0:2]))
                settle()
                for q in range(QB):
                    step(nc.vector.tensor_scalar(chosen0[:, q, :], iota, top_at_f[:, q, 0:1], None, ALU.is_equal))
                settle()
                for q in range(QB):
                    step(nc.vector.scalar_tensor_tensor(chosen[:, q, :], iota, top_at_f[:, q, 1:2], chosen0[:, q, :], ALU.is_equal, ALU.add))
                assert done[0] == CHOICE_OPS, done[0]

            def make_gates(c, par, between):
                done = [CHOICE_OPS]

                def step(ins):
                    done[0] += 1
                    ins.then_inc(gate_ops, 1)

                def settle():
                    between()
                    dve.wait_ge(gate_ops, GATE_OPS * c + done[0])

                dve.wait_ge(gate_ops, GATE_OPS * c + CHOICE_OPS)
                step(nc.vector.tensor_tensor(picked[:], chosen[:], scores[:], ALU.mult))
                settle()
                step(nc.vector.tensor_reduce(denom[:], picked[:], AX_X, ALU.add))
                settle()
                step(nc.vector.tensor_scalar(denom_eps[:], denom[:], 1e-9, None, ALU.add))
                step(nc.vector.tensor_scalar(denom_ok[:], denom[:], 1e-9, None, ALU.is_gt))
                settle()
                unit = H_SCALE / LAYER
                step(nc.vector.reciprocal(denom_inv[:], denom_eps[:]))
                step(nc.vector.tensor_scalar(gate_even[:], denom_ok[:], -0.5 * unit, 0.5 * unit, ALU.mult, ALU.add))
                settle()
                step(nc.vector.scalar_tensor_tensor(gate_scale[:], denom_inv[:], unit, denom_ok[:], ALU.mult, ALU.mult))
                settle()
                for q in range(QB):
                    step(nc.vector.tensor_scalar(gate_a[:, q, :], scores[:, q, :], gate_scale[:, q:q + 1], gate_even[:, q:q + 1], ALU.mult, ALU.add))
                settle()
                wait(dve, gates_stored, 16 * (c - 1))
                step(nc.vector.tensor_tensor(gates[par][:], gate_a[:], chosen[:], ALU.mult))
                assert done[0] == GATE_OPS, done[0]

            def tap(j, i):
                last = isinstance(j, int) and j == PAIRS - 1
                n = i + PE_TAP_OPS if last and i >= PE_FIRST_TAP else i
                k, kd = n // KD, n % KD
                window = hist[:, kd, k * B:k * B + PAIR]
                total = conv_part(kd, last)
                if k == 0:
                    if kd == 0:
                        dve.wait_ge(hist_moved, 2 * (j + 1))
                        wait(dve, conv_copied, 2 * j)
                    ins = nc.vector.tensor_scalar(total, window, cond[:, kd, 0:1], conv_bias[:, kd:kd + 1], ALU.mult, ALU.add)
                else:
                    if i == (PE_FIRST_TAP if last else KD * HIST_TAPS):
                        dve.wait_ge(hist_ready, j + 1)
                    dve.wait_ge(taps_done, TAP_OPS * j + i - KD + 1)
                    ins = nc.vector.scalar_tensor_tensor(total, window, cond[:, kd, k:k + 1], total, ALU.mult, ALU.add)
                ins.then_inc(taps_done, 1)

            by_time = lambda ap: ap.rearrange("p (t b) -> p t b", b=B)
            turned = lambda ap: ap[:].rearrange("p b t -> p t b")

            def driven(j, between):
                dve.wait_ge(post_act, 3 * (j + 1))
                nc.vector.scalar_tensor_tensor(b_t[:], z_b[:], 0.0, z_soft[:], ALU.max, ALU.add).then_inc(post_ops, 1)
                between()
                dve.wait_ge(post_ops, POST_OPS * j + 1)
                nc.vector.tensor_tensor(turned(drive), by_time(b_t[:]), by_time(u_t[:]), ALU.mult).then_inc(post_ops, 1)

            def scan(j, between):
                dve.wait_ge(post_ops, POST_OPS * j + 2)
                nc.vector.scalar_tensor_tensor(drive[:, :, 0], state[:, :, 2 * STEPS - 1], decay[:, 0:1], drive[:, :, 0], ALU.mult, ALU.add).then_inc(post_ops, 1)
                between()
                dve.wait_ge(post_ops, POST_OPS * j + 3)
                nc.vector.tensor_tensor_scan(state[:].rearrange("p b t -> p (b t)"), decay_run[:].rearrange("p b t -> p (b t)"),
                                             drive[:].rearrange("p b t -> p (b t)"), 0.0, ALU.mult, ALU.add).then_inc(post_ops, 1)

            def read_out(j):
                dve.wait_ge(post_ops, POST_OPS * j + 4)
                dve.wait_ge(post_copied, 3 * (2 * j + 2))
                wait(dve, out_sums, 2 * j)
                nc.vector.tensor_tensor(by_time(y_t[:]), by_time(c_t[:]), turned(state), ALU.mult).then_inc(post_ops, 1)

            def turn(t):
                _, scan_at, out_at = post_slots(t)
                for hf in range(2):
                    for m in range(UNITS):
                        s, slot = m - CHAIN_AT, UNITS * hf + m
                        if m == 1 and t.has(hf - 2):
                            c = t.chunk(hf - 2)
                            dve.wait_ge(router_sums, c + 1)
                            wait(dve, scored, c)
                            nc.vector.scalar_tensor_tensor(logits[:], ps_misc[:, 0, 0:QB * N_ROUTED].rearrange("p (q e) -> p q e", q=QB), 1.0 / W_SCALE,
                                                           cond_logits[:].rearrange("p (q e) -> p q e", q=1).broadcast_to((P, QB, N_ROUTED)), ALU.mult, ALU.add).then_inc(gate_ops, 1)
                        if m == LAG and t.has(hf - 3):
                            c = t.chunk(hf - 3)
                            dve.wait_ge(summed, UNITS * (c + 1))
                            wait(dve, hist_ready, t.i - 2 + hf)
                            nc.vector.scalar_tensor_tensor(x3_new[:, :, halves[1 - hf]], ps_y[:], Y_SCALE, x2[1 - hf][:], ALU.mult, ALU.add).then_inc(x3_done, 1)
                        if 0 <= s < STEPS and t.has(hf - 1):
                            spike_step(t.chunk(hf - 1), s, 1 - hf)
                        pair = t.i if isinstance(t.i, int) else 0
                        todo = [(t.i - 2, n) for n in taps_at(UNITS * hf + m, pair - 2)] if t.has_pair(-2) else []
                        if t.has_pair(-3):
                            todo = [(t.i - 3, n) for n in taps_at(UNITS * hf + m + 2 * UNITS, pair - 3)] + todo

                        def next_tap():
                            if todo:
                                tap(*todo.pop(0))

                        if m == 2 and t.has(hf - 2):
                            make_gates(t.chunk(hf - 2), hf, next_tap)
                        next_tap()
                        if m >= 1 and t.has(hf - 2) or m == 0 and t.has(hf - 3):
                            c = t.chunk(hf - 2) if m else t.chunk(hf - 3)
                            n = (m - 1) % UNITS
                            dve.wait_ge(hi_done, UNITS * c + n + 1)
                            nc.vector.tensor_tensor(hid_lo[n % SPLITS][:], hid[n % HIDS][:], hid_hi[n % SPLITS][:], ALU.subtract).then_inc(lo_done, 1)
                        if t.at(TURNS - 1) and hf == 0 and m == CONV_AT:
                            dve.wait_ge(tap_sums, PE_TAP_OPS)
                            dve.wait_ge(taps_done, TAP_OPS * PAIRS - PE_TAP_OPS)
                            dve.wait_ge(post_sums, CHUNKS - 2)
                            for kd in range(KD):
                                nc.vector.tensor_tensor(convolved[:, kd, :], conv_part(kd, True), flat(ps_hid[kd]), ALU.add).then_inc(conv_copied, 1)
                        if m == 1 and t.has(hf - 2):
                            choose_experts(t.chunk(hf - 2), next_tap)
                        if slot == scan_at and t.has_pair(-3):
                            driven(t.i - 3, next_tap)
                        if slot == scan_at + 1 and t.has_pair(-3):
                            scan(t.i - 3, next_tap)
                        if slot == scan_at + 2 and t.has_pair(-3):
                            read_out(t.i - 3)
                        while todo:
                            next_tap()
                        if m < SHARED_UNITS and t.has(hf - 2):
                            unit_evacuate(t.chunk(hf - 2), m, hf)
                        if t.at(0):
                            sums_with_spikes(nc.vector, t, hf, m)
                            sums_with_states(nc.vector, t, hf, m)
                        n = slot_stage(t, hf, m)
                        if n >= 0:
                            weight_stage(n)
                        if t.at(1) and hf == 1 and m == UNITS - 1:
                            last_layer_constants()
                        if slot - 1 in out_at and t.has_pair(-3):
                            j, q = t.i - 3, out_at.index(slot - 1)
                            dve.wait_ge(out_sums, 2 * j + q + 1)
                            wait(dve, out_stored, 16 * (2 * j))
                            at = HIST
                            if t.has_pair(-2):
                                dve.wait_ge(hist_ready, j + 2)
                                at = HIST - PAIR
                            for kd in range(KD):
                                nc.vector.scalar_tensor_tensor(out_sb[q][:, kd, :], ps_post(t, q)[:, kd, :], out_bias[:, kd:kd + 1],
                                                               hist[:, kd, at + q * TOK:at + (q + 1) * TOK], ALU.add, ALU.add).then_inc(out_done, 1)

            run_turns(dve, turn)

        @block.gpsimd
        def _(pool):
            pool.wait_ge(h_start, 1)

            def turn(t):
                for hf in range(2):
                    for m in range(UNITS):
                        s = m - CHAIN_AT
                        if t.at(1) and hf == 1 and m == 1:
                            pool.wait_ge(stage_hi, STAGES)
                            pool.wait_ge(stage_lo, STAGES)
                            nc.gpsimd.memset(hist[:], 0.0).then_inc(hist_zeroed, 1)
                        if m == 0 and t.has(hf):
                            pool.wait_ge(x_hi_done, t.chunk(hf) + 1)
                            nc.gpsimd.tensor_tensor(x_split[hf][1][:], x_in[hf][:], x_split[hf][0][:], ALU.subtract).then_inc(x_lo_done, 1)
                        if 0 <= s < STEPS and t.has(hf):
                            to, at = (hf, cols[s + 1]) if s < STEPS - 1 else (1 - hf, cols[0])
                            pool.wait_ge(h_ready, STEPS * t.chunk(hf) + s + 1)
                            nc.gpsimd.tensor_tensor(h_split[to][1][:, :, at], h_rnn[to][:, :, at], h_split[to][0][:, :, at], ALU.subtract).then_inc(h_lo_done, 1)
                        if not t.at(0):
                            sums_with_spikes(nc.gpsimd, t, hf, m)
                        if m >= SHARED_UNITS and t.has(hf - 2):
                            c = t.chunk(hf - 2)
                            e = m - SHARED_UNITS
                            if e == 0:
                                pool.wait_ge(gates_loaded[hf], 16 * t.i)
                            pool.wait_ge(activated, UNITS * c + m + 1)
                            gate = gates_all[hf][:, :, e:e + 1].rearrange("p n o -> p o n").broadcast_to((P, 2, TOK))
                            nc.gpsimd.tensor_tensor(hid[m % HIDS][:], hid[m % HIDS][:], gate, ALU.mult).then_inc(gated, 1)
                        if not t.at(0):
                            sums_with_states(nc.gpsimd, t, hf, m)

            run_turns(pool, turn)


def kernel(**inputs):
    import numpy as np
    import concourse.bacc as bacc
    from concourse.bass_utils import run_bass_kernel_spmd

    a = {k: np.asarray(v) for k, v in inputs.items()}

    def rows(w):
        n = w.shape[1]
        return w.reshape(-1, P, n).transpose(1, 0, 2).reshape(P, -1)

    def lay(v, width):
        full = np.zeros((P, width), np.float32)
        full[:v.shape[0], :v.shape[1]] = v
        return full

    c = a["cond_1024"]
    everywhere = lambda v: np.broadcast_to(v[None, :], (P, v.shape[0]))
    column = lambda v: v.reshape(-1, 1)
    alpha = a["L1_cond_alpha"]
    parts = {
        "wx": rows(a["L0_cond_Wx"].T), "wh": rows(a["L0_cond_Wh"].T), "cond": rows(c.T),
        "alpha_col": rows(np.broadcast_to(alpha[:, None], (D, B))),
        "w": rows(a["L1_cond_W"].T), "v": rows(a["L1_cond_V"]),
        "off_diag": rows(1.0 - np.eye(D, dtype=np.float32)), "alpha_row": everywhere(alpha),
        "cond4": rows(np.tile(c.T, (1, P // B))), "router": rows(a["L2_cond_W_router"].T),
        "router_bias": everywhere(np.tile(a["L2_cond_router_bias"], QB)),
        "iota": everywhere(np.arange(N_ROUTED, dtype=np.float32)),
        "proj": rows(a["L3_cond_Wp"]), "skip": rows(a["L3_cond_Ws"]), "out": lay(a["L3_cond_Wo"], D),
        "proj_bias": column(a["L3_cond_bp"]), "skip_bias": lay(column(a["L3_cond_bs"]), 1),
        "out_bias": rows(column(a["L3_cond_bo"])), "conv_bias": rows(column(a["L3_cond_conv_b"])),
        "logs": lay(np.stack([a["L3_cond_A_log"], a["L3_cond_dt_log"]], 1), 2),
    }
    small = np.ascontiguousarray(np.concatenate([parts[n] for n, _ in _SMALL], 1))
    experts = lambda w: np.concatenate([rows(w[e].T) for e in range(w.shape[0])], 1)
    big = np.ascontiguousarray(np.concatenate(
        [experts(a[f"L2_cond_{n}"]) for n in ("s_w1", "s_w3", "s_w2", "r_w1", "r_w2")], 1))
    x = np.ascontiguousarray(a["x"].transpose(2, 1, 0).reshape(KD, P, T * B).transpose(1, 0, 2))

    nc = bacc.Bacc("TRN2", target_bir_lowering=False, num_devices=1)
    arrays = {"x_t": x, "small_w": small, "big_w": big}
    args = [nc.dram_tensor(n, v.shape, F32, kind="ExternalInput").ap() for n, v in arrays.items()]
    args.append(nc.dram_tensor("out_t", (P, KD, T * B), F32, kind="ExternalOutput").ap())
    args.append(nc.dram_tensor("gates_scratch", (2, TOK, N_ROUTED), F32, kind="Internal").ap())
    build(nc, *args)
    r = run_bass_kernel_spmd(nc, [arrays], core_ids=[0])
    y = r.results[0]["out_t"]
    return np.ascontiguousarray(y.transpose(1, 0, 2).reshape(D, T, B).transpose(2, 1, 0))
```
